# Optimizing a Trainium2 kernel written in Bass

```python
import numpy as np
import jax
import jax.numpy as jnp

def _softmax(x, axis=-1):
    return jax.nn.softmax(x, axis=axis)

def _gelu(x):
    return jax.nn.gelu(x, approximate=True)

def _silu(x):
    return jax.nn.silu(x)

def _sigmoid(x):
    return jax.nn.sigmoid(x)

def _layernorm(x, axis=-1, eps=1e-05):
    m = jnp.mean(x, axis=axis, keepdims=True)
    v = jnp.var(x, axis=axis, keepdims=True)
    return (x - m) / jnp.sqrt(v + eps)

def _scatter_add(tgt, idx, src, axis=0):
    return tgt.at[idx].add(src)

def _segment_sum(src, seg, n):
    return jax.ops.segment_sum(src, seg, n)
kernel_name = 'mk_perceiver_d2_seqx_r2_315e98'

def setup_inputs(seed: int=0):
    np.random.seed(seed)
    _w = jnp.asarray

    def _rec_inputs():
        import jax
        import jax.numpy as jnp
        _rk = jax.random.key(seed)
        x = -0.0005207 + 1.001 * jax.random.normal(jax.random.fold_in(_rk, 1), (2, 128, 512), jnp.float32)
        _lenS = 128 - jax.random.randint(jax.random.fold_in(_rk, 7), (2,), 0, max(1, 128 // 4) + 1, jnp.int32)
        _lenS2 = 2048 - jax.random.randint(jax.random.fold_in(_rk, 8), (2,), 0, max(1, 2048 // 4) + 1, jnp.int32)
        _ctx_1024P = jax.random.normal(jax.random.fold_in(_rk, 11), (2, 16, 512), jnp.float32)
        _ctx_1024c = jax.random.dirichlet(jax.random.fold_in(_rk, 511), 0.3 * jnp.ones((16,), jnp.float32), (2, 2048))
        _ctx_1024t = jnp.einsum('bsk,bkd->bsd', _ctx_1024c, _ctx_1024P)
        _ctx_1024t = _ctx_1024t * jax.lax.rsqrt(jnp.mean(jnp.square(_ctx_1024t)) + 1e-12) * 0.953939
        ctx_1024 = -1.52775e-05 + 0.999936 * (_ctx_1024t + 0.3 * jax.random.normal(jax.random.fold_in(_rk, 611), (2, 2048, 512), jnp.float32))
        return (x, ctx_1024)
    x, ctx_1024 = _rec_inputs()

    def _L0_xattn_setup():
        import jax, jax.numpy as jnp
        import numpy as np
        DIM = 512
        HEADS = 16
        DHEAD = 64
        INNER = HEADS * DHEAD
        EPS = 1e-05

        def layer_norm(x, g, b):
            mu = jnp.mean(x, axis=-1, keepdims=True)
            var = jnp.mean(jnp.square(x - mu), axis=-1, keepdims=True)
            return (x - mu) * jax.lax.rsqrt(var + EPS) * g + b

        def apply_rope(x, cos, sin):
            d2 = x.shape[-1] // 2
            x1, x2 = (x[..., :d2], x[..., d2:])
            return jnp.concatenate([x1 * cos - x2 * sin, x2 * cos + x1 * sin], axis=-1)
        key = jax.random.key(seed)
        ks = jax.random.split(key, 10)
        B, N, S = (8, 128, 2048)
        latents = jax.random.normal(ks[0], (B, N, DIM), dtype=jnp.float32)
        context = jax.random.normal(ks[1], (B, S, DIM), dtype=jnp.float32)
        cos = jax.random.uniform(ks[2], (S, DHEAD // 2), dtype=jnp.float32)
        sin = jax.random.uniform(ks[3], (S, DHEAD // 2), dtype=jnp.float32)
        init = lambda k, shp, fan_in: jax.random.normal(k, shp, dtype=jnp.float32) / np.sqrt(fan_in)
        return {'latents': latents, 'context': context, 'cos': cos, 'sin': sin, 'ln_lat_g': jnp.ones((DIM,), jnp.float32), 'ln_lat_b': jnp.zeros((DIM,), jnp.float32), 'ln_ctx_g': jnp.ones((DIM,), jnp.float32), 'ln_ctx_b': jnp.zeros((DIM,), jnp.float32), 'Wq': init(ks[4], (DIM, INNER), DIM), 'Wkv': init(ks[5], (DIM, 2 * INNER), DIM), 'Wo': init(ks[6], (INNER, DIM), INNER), 'bo': jnp.zeros((DIM,), jnp.float32)}
    _L0_xattn_all = _L0_xattn_setup()
    _L0_xattn_in = {k: v for k, v in _L0_xattn_all.items() if k in ('cos', 'sin', 'ln_lat_g', 'ln_lat_b', 'ln_ctx_g', 'ln_ctx_b', 'Wq', 'Wkv', 'Wo', 'bo')}
    del _L0_xattn_all

    def _L0_attn_setup():
        import jax, jax.numpy as jnp
        import numpy as np
        N_INPUT = 512
        N_HEAD = 16
        ATT_DIM = N_INPUT // N_HEAD * N_HEAD
        V_DIM = N_INPUT // 2 * N_HEAD
        COMB_DIM = 2 * ATT_DIM + V_DIM
        SCALE = (N_INPUT // N_HEAD) ** 0.5
        key = jax.random.key(seed)
        k1, k2, k3 = jax.random.split(key, 3)
        B, T = (8, 512)
        representations = jax.random.normal(k1, (B, T, N_INPUT), dtype=jnp.float32)
        Wc = jax.random.normal(k2, (COMB_DIM, N_INPUT), dtype=jnp.float32) * (0.1 * np.sqrt(2.0 / (COMB_DIM + N_INPUT)))
        bc = jnp.zeros((COMB_DIM,), dtype=jnp.float32)
        Wo = jax.random.normal(k3, (N_INPUT, V_DIM), dtype=jnp.float32) * (0.1 * np.sqrt(2.0 / (N_INPUT + V_DIM)))
        bo = jnp.zeros((N_INPUT,), dtype=jnp.float32)
        return {'representations': representations, 'Wc': Wc, 'bc': bc, 'Wo': Wo, 'bo': bo}
    _L0_attn_all = _L0_attn_setup()
    _L0_attn_in = {k: v for k, v in _L0_attn_all.items() if k in ('Wc', 'bc', 'Wo', 'bo')}
    del _L0_attn_all

    def _L0_ffn_setup():
        import jax, jax.numpy as jnp
        import numpy as np
        B, S, D = (1, 1024, 512)
        I = 1024
        E = 8
        K = 2
        LIMIT = 7.0
        ALPHA = 1.702
        EPS = 1e-05

        def _swiglu(h):
            x_glu = jnp.minimum(h[..., ::2], LIMIT)
            x_lin = jnp.clip(h[..., 1::2], -LIMIT, LIMIT)
            return x_glu * jax.nn.sigmoid(ALPHA * x_glu) * (x_lin + 1.0)

        def _moe(t, gate_w, gate_b, mlp1_w, mlp1_b, mlp2_w, mlp2_b):
            T = t.shape[0]
            logits = t @ gate_w + gate_b
            top_v, top_i = jax.lax.top_k(logits, K)
            probs = jax.nn.softmax(top_v, axis=-1)
            w = jnp.zeros((T, E), t.dtype).at[jnp.arange(T)[:, None], top_i].set(probs)

            def body(acc, ew):
                w1, b1, w2, b2, we = ew
                h = _swiglu(t @ w1 + b1)
                y = h @ w2 + b2
                return (acc + we[:, None] * y, None)
            acc0 = jnp.zeros((T, t.shape[1]), t.dtype)
            acc, _ = jax.lax.scan(body, acc0, (mlp1_w, mlp1_b, mlp2_w, mlp2_b, w.T))
            return acc
        key = jax.random.key(seed)
        ks = jax.random.split(key, 4)
        s = 0.02
        return {'x': jax.random.normal(ks[0], (B, S, D), jnp.float32), 'norm_scale': jnp.ones((D,), jnp.float32), 'gate_w': jax.random.normal(ks[1], (D, E), jnp.float32) * s, 'gate_b': jnp.zeros((E,), jnp.float32), 'mlp1_w': jax.random.normal(ks[2], (E, D, 2 * I), jnp.float32) * s, 'mlp1_b': jnp.zeros((E, 2 * I), jnp.float32), 'mlp2_w': jax.random.normal(ks[3], (E, I, D), jnp.float32) * s, 'mlp2_b': jnp.zeros((E, D), jnp.float32)}
    _L0_ffn_all = _L0_ffn_setup()
    _L0_ffn_in = {k: v for k, v in _L0_ffn_all.items() if k in ('norm_scale', 'gate_w', 'gate_b', 'mlp1_w', 'mlp1_b', 'mlp2_w', 'mlp2_b')}
    del _L0_ffn_all

    def _L1_xattn_setup():
        import jax, jax.numpy as jnp
        import numpy as np
        D_MODEL = 512
        NUM_HEADS = 16
        D_K = D_MODEL // NUM_HEADS
        key = jax.random.key(seed)
        ks = jax.random.split(key, 11)
        B, S = (2, 1024)
        scale = 1.0 / np.sqrt(D_MODEL)
        inp = {'q': jax.random.normal(ks[0], (B, S, D_MODEL), jnp.float32), 'k': jax.random.normal(ks[1], (B, S, D_MODEL), jnp.float32), 'v': jax.random.normal(ks[2], (B, S, D_MODEL), jnp.float32), 'Wq': jax.random.normal(ks[3], (D_MODEL, D_MODEL), jnp.float32) * scale, 'bq': jnp.zeros((D_MODEL,), jnp.float32), 'Wk': jax.random.normal(ks[4], (D_MODEL, D_MODEL), jnp.float32) * scale, 'bk': jnp.zeros((D_MODEL,), jnp.float32), 'Wv': jax.random.normal(ks[5], (D_MODEL, D_MODEL), jnp.float32) * scale, 'bv': jnp.zeros((D_MODEL,), jnp.float32), 'Wo': jax.random.normal(ks[6], (D_MODEL, D_MODEL), jnp.float32) * scale, 'bo': jnp.zeros((D_MODEL,), jnp.float32)}
        return inp
    _L1_xattn_all = _L1_xattn_setup()
    _L1_xattn_in = {k: v for k, v in _L1_xattn_all.items() if k in ('Wq', 'bq', 'Wk', 'bk', 'Wv', 'bv', 'Wo', 'bo')}
    del _L1_xattn_all

    def _L1_attn_setup():
        import jax, jax.numpy as jnp
        import numpy as np
        HEADS = 64
        DIM_HEAD = 64
        SCALE = DIM_HEAD ** (-0.5)
        EPS = 1e-06
        key = jax.random.key(seed)
        ks = jax.random.split(key, 6)
        b, s, dim = (2, 2048, 512)
        inner = HEADS * DIM_HEAD
        std = 0.02
        return {'x': jax.random.normal(ks[0], (b, s, dim), dtype=jnp.float32), 'Wq': jax.random.normal(ks[1], (dim, inner), dtype=jnp.float32) * std, 'Wk': jax.random.normal(ks[2], (dim, inner), dtype=jnp.float32) * std, 'Wv': jax.random.normal(ks[3], (dim, inner), dtype=jnp.float32) * std, 'Wo': jax.random.normal(ks[4], (inner, dim), dtype=jnp.float32) * std, 'bo': jnp.zeros((dim,), dtype=jnp.float32)}
    _L1_attn_all = _L1_attn_setup()
    _L1_attn_in = {k: v for k, v in _L1_attn_all.items() if k in ('Wq', 'Wk', 'Wv', 'Wo', 'bo')}
    del _L1_attn_all

    def _L1_ffn_setup():
        import jax, jax.numpy as jnp
        import numpy as np
        B, S, H, E, DFF = (4, 2048, 512, 8, 2048)
        key = jax.random.key(seed)
        k0, k1, k2, k3 = jax.random.split(key, 4)
        hidden_states = jax.random.normal(k0, (B, S, H), dtype=jnp.float32)
        gate_w = jax.random.normal(k1, (E, H), dtype=jnp.float32) * 0.02
        w1 = jax.random.normal(k2, (E, H, DFF), dtype=jnp.float32) * 0.02
        b1 = jnp.zeros((E, DFF), dtype=jnp.float32)
        w2 = jax.random.normal(k3, (E, DFF, H), dtype=jnp.float32) * 0.02
        b2 = jnp.zeros((E, H), dtype=jnp.float32)
        return {'hidden_states': hidden_states, 'gate_w': gate_w, 'w1': w1, 'b1': b1, 'w2': w2, 'b2': b2}
    _L1_ffn_all = _L1_ffn_setup()
    _L1_ffn_in = {k: v for k, v in _L1_ffn_all.items() if k in ('gate_w', 'w1', 'b1', 'w2', 'b2')}
    del _L1_ffn_all
    return {'x': x, 'ctx_1024': ctx_1024, 'L0_xattn_cos': _L0_xattn_in['cos'], 'L0_xattn_sin': _L0_xattn_in['sin'], 'L0_xattn_ln_lat_g': _L0_xattn_in['ln_lat_g'], 'L0_xattn_ln_lat_b': _L0_xattn_in['ln_lat_b'], 'L0_xattn_ln_ctx_g': _L0_xattn_in['ln_ctx_g'], 'L0_xattn_ln_ctx_b': _L0_xattn_in['ln_ctx_b'], 'L0_xattn_Wq': _L0_xattn_in['Wq'], 'L0_xattn_Wkv': _L0_xattn_in['Wkv'], 'L0_xattn_Wo': _L0_xattn_in['Wo'], 'L0_xattn_bo': _L0_xattn_in['bo'], 'L0_attn_Wc': _L0_attn_in['Wc'], 'L0_attn_bc': _L0_attn_in['bc'], 'L0_attn_Wo': _L0_attn_in['Wo'], 'L0_attn_bo': _L0_attn_in['bo'], 'L0_ffn_norm_scale': _L0_ffn_in['norm_scale'], 'L0_ffn_gate_w': _L0_ffn_in['gate_w'], 'L0_ffn_gate_b': _L0_ffn_in['gate_b'], 'L0_ffn_mlp1_w': _L0_ffn_in['mlp1_w'], 'L0_ffn_mlp1_b': _L0_ffn_in['mlp1_b'], 'L0_ffn_mlp2_w': _L0_ffn_in['mlp2_w'], 'L0_ffn_mlp2_b': _L0_ffn_in['mlp2_b'], 'L1_xattn_Wq': _L1_xattn_in['Wq'], 'L1_xattn_bq': _L1_xattn_in['bq'], 'L1_xattn_Wk': _L1_xattn_in['Wk'], 'L1_xattn_bk': _L1_xattn_in['bk'], 'L1_xattn_Wv': _L1_xattn_in['Wv'], 'L1_xattn_bv': _L1_xattn_in['bv'], 'L1_xattn_Wo': _L1_xattn_in['Wo'], 'L1_xattn_bo': _L1_xattn_in['bo'], 'L1_attn_Wq': _L1_attn_in['Wq'], 'L1_attn_Wk': _L1_attn_in['Wk'], 'L1_attn_Wv': _L1_attn_in['Wv'], 'L1_attn_Wo': _L1_attn_in['Wo'], 'L1_attn_bo': _L1_attn_in['bo'], 'L1_ffn_gate_w': _L1_ffn_in['gate_w'], 'L1_ffn_w1': _L1_ffn_in['w1'], 'L1_ffn_b1': _L1_ffn_in['b1'], 'L1_ffn_w2': _L1_ffn_in['w2'], 'L1_ffn_b2': _L1_ffn_in['b2']}

def reference(x, ctx_1024, L0_xattn_cos, L0_xattn_sin, L0_xattn_ln_lat_g, L0_xattn_ln_lat_b, L0_xattn_ln_ctx_g, L0_xattn_ln_ctx_b, L0_xattn_Wq, L0_xattn_Wkv, L0_xattn_Wo, L0_xattn_bo, L0_attn_Wc, L0_attn_bc, L0_attn_Wo, L0_attn_bo, L0_ffn_norm_scale, L0_ffn_gate_w, L0_ffn_gate_b, L0_ffn_mlp1_w, L0_ffn_mlp1_b, L0_ffn_mlp2_w, L0_ffn_mlp2_b, L1_xattn_Wq, L1_xattn_bq, L1_xattn_Wk, L1_xattn_bk, L1_xattn_Wv, L1_xattn_bv, L1_xattn_Wo, L1_xattn_bo, L1_attn_Wq, L1_attn_Wk, L1_attn_Wv, L1_attn_Wo, L1_attn_bo, L1_ffn_gate_w, L1_ffn_w1, L1_ffn_b1, L1_ffn_w2, L1_ffn_b2):
    import jax
    import jax.numpy as jnp

    def _L0_xattn_ref(latents, context, cos, sin, ln_lat_g, ln_lat_b, ln_ctx_g, ln_ctx_b, Wq, Wkv, Wo, bo):
        import jax, jax.numpy as jnp
        import numpy as np
        DIM = 512
        HEADS = 16
        DHEAD = 64
        INNER = HEADS * DHEAD
        EPS = 1e-05

        def layer_norm(x, g, b):
            mu = jnp.mean(x, axis=-1, keepdims=True)
            var = jnp.mean(jnp.square(x - mu), axis=-1, keepdims=True)
            return (x - mu) * jax.lax.rsqrt(var + EPS) * g + b

        def apply_rope(x, cos, sin):
            d2 = x.shape[-1] // 2
            x1, x2 = (x[..., :d2], x[..., d2:])
            return jnp.concatenate([x1 * cos - x2 * sin, x2 * cos + x1 * sin], axis=-1)
        b, n, _ = latents.shape
        s = context.shape[1]
        lat = layer_norm(latents, ln_lat_g, ln_lat_b)
        ctx = layer_norm(context, ln_ctx_g, ln_ctx_b)
        q = (lat @ Wq).reshape(b, n, HEADS, DHEAD).transpose(0, 2, 1, 3)
        kv = ctx @ Wkv
        k, v = jnp.split(kv, 2, axis=-1)
        k = k.reshape(b, s, HEADS, DHEAD).transpose(0, 2, 1, 3)
        v = v.reshape(b, s, HEADS, DHEAD).transpose(0, 2, 1, 3)
        k = apply_rope(k, cos[None, None], sin[None, None])
        scale = DHEAD ** (-0.5)
        attn = jnp.einsum('bhnd,bhsd->bhns', q, k) * scale
        attn = jnp.clip(attn, -11.0, 11.0)
        attn = jax.nn.softmax(attn, axis=-1)
        out = jnp.einsum('bhns,bhsd->bhnd', attn, v)
        out = out.transpose(0, 2, 1, 3).reshape(b, n, INNER)
        return out @ Wo + bo

    def _L0_attn_ref(representations, Wc, bc, Wo, bo):
        import jax, jax.numpy as jnp
        import numpy as np
        N_INPUT = 512
        N_HEAD = 16
        ATT_DIM = N_INPUT // N_HEAD * N_HEAD
        V_DIM = N_INPUT // 2 * N_HEAD
        COMB_DIM = 2 * ATT_DIM + V_DIM
        SCALE = (N_INPUT // N_HEAD) ** 0.5
        B, T, D = representations.shape
        H = N_HEAD
        dh = ATT_DIM // H
        dv = V_DIM // H
        cp = jax.nn.leaky_relu(jnp.einsum('btd,cd->btc', representations, Wc) + bc)
        q = cp[..., :ATT_DIM].reshape(B, T, H, dh)
        k = cp[..., ATT_DIM:2 * ATT_DIM].reshape(B, T, H, dh)
        v = cp[..., 2 * ATT_DIM:].reshape(B, T, H, dv)
        scores = jnp.einsum('bqhd,bkhd->bhqk', q, k) / SCALE
        attn = jax.nn.softmax(scores, axis=-1)
        out = jnp.einsum('bhqk,bkhd->bqhd', attn, v).reshape(B, T, V_DIM)
        proj = jax.nn.leaky_relu(jnp.einsum('btv,dv->btd', out, Wo) + bo)
        return representations + proj

    def _L0_ffn_ref(x, norm_scale, gate_w, gate_b, mlp1_w, mlp1_b, mlp2_w, mlp2_b):
        import jax, jax.numpy as jnp
        import numpy as np
        B, S, D = (1, 1024, 512)
        I = 1024
        E = 8
        K = 2
        LIMIT = 7.0
        ALPHA = 1.702
        EPS = 1e-05

        def _swiglu(h):
            x_glu = jnp.minimum(h[..., ::2], LIMIT)
            x_lin = jnp.clip(h[..., 1::2], -LIMIT, LIMIT)
            return x_glu * jax.nn.sigmoid(ALPHA * x_glu) * (x_lin + 1.0)

        def _moe(t, gate_w, gate_b, mlp1_w, mlp1_b, mlp2_w, mlp2_b):
            T = t.shape[0]
            logits = t @ gate_w + gate_b
            top_v, top_i = jax.lax.top_k(logits, K)
            probs = jax.nn.softmax(top_v, axis=-1)
            w = jnp.zeros((T, E), t.dtype).at[jnp.arange(T)[:, None], top_i].set(probs)

            def body(acc, ew):
                w1, b1, w2, b2, we = ew
                h = _swiglu(t @ w1 + b1)
                y = h @ w2 + b2
                return (acc + we[:, None] * y, None)
            acc0 = jnp.zeros((T, t.shape[1]), t.dtype)
            acc, _ = jax.lax.scan(body, acc0, (mlp1_w, mlp1_b, mlp2_w, mlp2_b, w.T))
            return acc
        Bx, Sx, Dx = x.shape
        ms = jnp.mean(x * x, axis=-1, keepdims=True)
        t = (x * jax.lax.rsqrt(ms + EPS) * norm_scale).reshape(Bx * Sx, Dx)
        y = _moe(t, gate_w, gate_b, mlp1_w, mlp1_b, mlp2_w, mlp2_b)
        return x + y.reshape(Bx, Sx, Dx)

    def _L1_xattn_ref(q, k, v, Wq, bq, Wk, bk, Wv, bv, Wo, bo):
        import jax, jax.numpy as jnp
        import numpy as np
        D_MODEL = 512
        NUM_HEADS = 16
        D_K = D_MODEL // NUM_HEADS
        B, S, _ = q.shape
        H, Dk = (NUM_HEADS, D_K)

        def proj(x, W, b):
            y = x @ W + b
            return y.reshape(B, -1, H, Dk).transpose(0, 2, 1, 3)
        qh = proj(q, Wq, bq)
        kh = proj(k, Wk, bk)
        vh = proj(v, Wv, bv)
        scores = jnp.einsum('bhqd,bhkd->bhqk', qh, kh) / jnp.sqrt(jnp.float32(Dk))
        weights = jax.nn.softmax(scores, axis=-1)
        x = jnp.einsum('bhqk,bhkd->bhqd', weights, vh)
        x = x.transpose(0, 2, 1, 3).reshape(B, S, D_MODEL)
        return x @ Wo + bo

    def _L1_attn_ref(x, Wq, Wk, Wv, Wo, bo):
        import jax, jax.numpy as jnp
        import numpy as np
        HEADS = 64
        DIM_HEAD = 64
        SCALE = DIM_HEAD ** (-0.5)
        EPS = 1e-06
        b, s, dim = x.shape
        h, dh = (HEADS, DIM_HEAD)
        q = (x @ Wq).reshape(b, s, h, dh)
        k = (x @ Wk).reshape(b, s, h, dh)
        v = (x @ Wv).reshape(b, s, h, dh)
        q = jax.nn.relu(q) * SCALE
        k = jax.nn.relu(k)
        kv = jnp.einsum('bsid,bsjd->bsdj', k, v)
        out = jnp.einsum('bsid,bsdj->bsij', q, kv)
        q_norm = jnp.einsum('bsid,bsd->bsi', q, k.sum(axis=2))
        out = out / (q_norm[..., None] + EPS)
        out = out.reshape(b, s, h * h)
        return out @ Wo + bo

    def _L1_ffn_ref(hidden_states, gate_w, w1, b1, w2, b2):
        import jax, jax.numpy as jnp
        import numpy as np
        B, S, H, E, DFF = (4, 2048, 512, 8, 2048)
        b, s, h = hidden_states.shape
        x = hidden_states.reshape(-1, h)
        gate_logits = x @ gate_w.T
        gate_probs = jax.nn.softmax(gate_logits, axis=-1)
        expert_idx = jnp.argmax(gate_probs, axis=-1)
        expert_w = jnp.take_along_axis(gate_probs, expert_idx[:, None], axis=1)[:, 0]
        out = jnp.zeros_like(x)
        n_experts = w1.shape[0]
        for e in range(n_experts):
            ye = jax.nn.relu(x @ w1[e] + b1[e]) @ w2[e] + b2[e]
            sel = (expert_idx == e)[:, None]
            out = out + jnp.where(sel, ye * expert_w[:, None], 0.0)
        return out.reshape(b, s, h)
    x = x + _L0_xattn_ref(_layernorm(x, axis=-1), ctx_1024, L0_xattn_cos, L0_xattn_sin, L0_xattn_ln_lat_g, L0_xattn_ln_lat_b, L0_xattn_ln_ctx_g, L0_xattn_ln_ctx_b, L0_xattn_Wq, L0_xattn_Wkv, L0_xattn_Wo, L0_xattn_bo)
    x = x + _L0_attn_ref(_layernorm(x, axis=-1), L0_attn_Wc, L0_attn_bc, L0_attn_Wo, L0_attn_bo)
    x = x + _L0_ffn_ref(_layernorm(x, axis=-1), L0_ffn_norm_scale, L0_ffn_gate_w, L0_ffn_gate_b, L0_ffn_mlp1_w, L0_ffn_mlp1_b, L0_ffn_mlp2_w, L0_ffn_mlp2_b)
    x = x + _L1_xattn_ref(_layernorm(x, axis=-1), ctx_1024, ctx_1024, L1_xattn_Wq, L1_xattn_bq, L1_xattn_Wk, L1_xattn_bk, L1_xattn_Wv, L1_xattn_bv, L1_xattn_Wo, L1_xattn_bo)
    x = x + _L1_attn_ref(_layernorm(x, axis=-1), L1_attn_Wq, L1_attn_Wk, L1_attn_Wv, L1_attn_Wo, L1_attn_bo)
    x = x + _L1_ffn_ref(_layernorm(x, axis=-1), L1_ffn_gate_w, L1_ffn_w1, L1_ffn_b1, L1_ffn_w2, L1_ffn_b2)
    return x

_drawn_inputs = setup_inputs


def setup_inputs(seed=0):
    import zlib

    import numpy as np

    out = dict(_drawn_inputs(seed))
    spreads = {'L0_xattn_ln_lat_g': (1.0, 0.6),
     'L0_xattn_ln_lat_b': (0.0, 0.541),
     'L0_xattn_ln_ctx_g': (1.0, 0.2),
     'L0_xattn_ln_ctx_b': (0.0, 0.1),
     'L0_xattn_bo': (0.0, 0.1),
     'L0_attn_bc': (0.0, 0.8),
     'L0_attn_bo': (0.0, 0.289),
     'L0_ffn_norm_scale': (1.0, 0.6),
     'L0_ffn_gate_b': (0.0, 0.352),
     'L0_ffn_mlp1_b': (0.0, 0.761),
     'L0_ffn_mlp2_b': (0.0, 0.348),
     'L1_xattn_bq': (0.0, 0.8),
     'L1_xattn_bk': (0.0, 0.8),
     'L1_xattn_bv': (0.0, 0.1),
     'L1_xattn_bo': (0.0, 0.1),
     'L1_attn_bo': (0.0, 0.267),
     'L1_ffn_b1': (0.0, 0.8),
     'L1_ffn_b2': (0.0, 0.8)}
    factors = {'L0_xattn_cos': 7.407,
     'L0_xattn_sin': 7.302,
     'L0_attn_Wc': 8.0,
     'L0_attn_Wo': 8.0,
     'L1_attn_Wk': 7.605}
    for name, (base, spread) in spreads.items():
        noise = np.random.default_rng([zlib.crc32(name.encode()), seed]).standard_normal(out[name].shape)
        drawn = base * np.exp(spread * noise) if base else spread * noise
        out[name] = jnp.asarray(drawn.astype(out[name].dtype))
    for name, factor in factors.items():
        out[name] = (out[name] * factor).astype(out[name].dtype)
    return out
```

```python
from contextlib import ExitStack

import concourse.bass as bass
from concourse import mybir
from concourse.alu_op_type import AluOpType as ALU

F32 = mybir.dt.float32
F32R = mybir.dt.float32r
U32 = mybir.dt.uint32
ACT = mybir.ActivationFunctionType
AX = mybir.AxisListType

P = 128
D = 512
KC = D // P
B = 2
T = B * P
S = 2048
EPS = 1e-5
RAW = 4
SPLIT = 2
E = 8
GLANCE = 4

X0_WQ, X0_WK, X0_WV, X0_WO = 0, 2, 4, 6
A0_WQK, A0_WV, A0_WO = 8, 10, 18
F0_W = 26
X1_WQ, X1_WK, X1_WV, X1_WO = 74, 75, 76, 77
A1_WK, A1_WQ, A1_WV, A1_WO = 78, 86, 94, 102
F1_W = 110
TILES = 174
RESIDENT = 2


class Chain:

    def __init__(self, engine, sem):
        self.engine, self.sem, self.base, self.local = engine, sem, 0, 0

    def done(self, instruction):
        instruction.then_inc(self.sem, 1)
        self.local += 1

    def wait(self):
        self.engine.wait_ge(self.sem, self.base + self.local)

    def step(self, instruction):
        self.done(instruction)
        self.wait()

    def enter(self, i, per_iteration):
        self.outer, self.base = self.base + self.local, self.base + self.local + i * per_iteration
        self.per, self.local = per_iteration, 0

    def leave(self, passes):
        assert self.local == self.per, (self.local, self.per)
        self.base, self.local = self.outer + passes * self.per, 0


class Core:

    def __init__(self, nc, ctx, dram):
        self.nc, self.ctx, self.dram = nc, ctx, dram

        def sb(name, shape, dt=F32):
            return ctx.enter_context(nc.sbuf_tensor(name, shape, dt))

        def sem(name):
            return ctx.enter_context(nc.semaphore(name))

        self.raw = sb("raw", [P, RAW, KC, D])
        self.w_hi = sb("w_hi", [P, SPLIT, KC, D], F32R)
        self.w_lo = sb("w_lo", [P, SPLIT, KC, D], F32R)
        self.ident = sb("ident", [P, P])
        self.x = sb("residual", [P, B, D])
        self.a = sb("normed", [P, B, D])
        self.xt_hi = sb("xt_hi", [P, KC, T], F32R)
        self.xt_lo = sb("xt_lo", [P, KC, T], F32R)
        self.eps = sb("eps", [P, 2])
        self.psum = ctx.enter_context(nc.psum_tensor("psum", [P, 8, 512], F32))

        self.raw_ready = [sem(f"raw_ready{i}") for i in range(RAW)]
        self.hi_ready = sem("hi_ready")
        self.lo_ready = sem("lo_ready")
        self.w_used = sem("w_used")
        self.const_ready = sem("const_ready")
        self.x_loaded = sem("x_loaded")
        self.seen = [sem(f"seen{b}") for b in range(B)]
        self.context_loads = dram["ctx"].rearrange("b (g j p) d -> b g p j d", p=P, j=GLANCE)

        self.layer_sems = []
        self.act_own = sem("act_own")
        self.dve_own = sem("dve_own")
        self.pool_own = sem("pool_own")
        self.act_chain = Chain(nc.scalar, self.act_own)
        self.dve_chain = Chain(nc.vector, self.dve_own)
        self.pool_chain = Chain(nc.gpsimd, self.pool_own)

    def layer_sem(self, name):
        self.layer_sems.append(self.nc.alloc_semaphore(name=name))
        return self.layer_sems[-1]

    def free_semaphores(self):
        self.nc.clear_and_free_semaphores(self.layer_sems)
        self.nc.all_engine_barrier()
        self.layer_sems = []


    def load_weight(self, eng, first, i=0):
        if first >= RAW:
            eng.wait_ge(self.lo_ready, i + (first - RAW + 1))
        tile = self.dram["weights"]
        src = tile[first] if isinstance(i, int) else tile[bass.ds(i + first, 1)].rearrange("a p n -> (a p) n")
        eng.dma_start(self.raw[:, first % RAW].rearrange("p k n -> p (k n)"), src)\
           .then_inc(self.raw_ready[first % RAW], 16)

    def split_hi(self, act, first, i=0, to=None):
        act.wait_ge(self.raw_ready[first % RAW], i * (16 // RAW) + 16 * (first // RAW + 1))
        if to is None:
            n = first - RESIDENT if first >= X0_WV else first
            if n >= SPLIT:
                act.wait_ge(self.w_used, i + (n - SPLIT + 1))
            to = self.w_hi[:, n % SPLIT]
        act.copy(to, self.raw[:, first % RAW]).then_inc(self.hi_ready, 1)

    def split_lo(self, dve, first, i=0, to=None, hi=None):
        dve.wait_ge(self.hi_ready, i + (first + 1))
        if to is None:
            n = first - RESIDENT if first >= X0_WV else first
            to, hi = self.w_lo[:, n % SPLIT], self.w_hi[:, n % SPLIT]
        dve.tensor_tensor(to, self.raw[:, first % RAW], hi.bitcast(F32), ALU.subtract)\
           .then_inc(self.lo_ready, 1)

    def wait_products(self, eng, first, i=0):
        eng.wait_ge(self.w_used, i + ((first - RESIDENT if first >= X0_WV else first) + 1))

    def slot(self, first):
        return (first - RESIDENT if first >= X0_WV else first) % SPLIT


def three_passes(pe, out, lhs, rhs, first=True, last=True):
    pe.matmul(out, lhs[0], rhs[0], start=first, stop=False)
    pe.matmul(out, lhs[0], rhs[1], start=False, stop=False)
    return pe.matmul(out, lhs[1], rhs[0], start=False, stop=last)
def constants(c, glance, n0_col, n0_cols):
    nc = c.nc
    with nc.Block(no_gpsimd_drain=True) as block:

        @block.sync
        def _(sp):
            sp.dma_start(c.x[:], c.dram["x"].rearrange("b p d -> p b d")).then_inc(c.x_loaded, 16)
            for n, name in enumerate(("ln_lat_g", "ln_lat_b")):
                sp.dma_start(n0_col[:, n, :], c.dram[name]).then_inc(n0_cols, 16)
            for t in range(RAW):
                if t < B:
                    sp.dma_start(glance[:, t], c.context_loads[t, 0]).then_inc(c.seen[t], 16)
                c.load_weight(sp, t)

        @block.gpsimd
        def _(pool):
            c.pool_chain.step(pool.memset(c.ident[:], 0.0))
            pool.affine_select(out=c.ident[:], in_=c.ident[:], compare_op=ALU.not_equal, fill=1.0, base=0,
                               pattern=[[-1, P]], channel_multiplier=1).then_inc(c.const_ready, 1)

        @block.vector
        def _(dve):
            dve.memset(c.eps[:], EPS).then_inc(c.const_ready, 1)
            dve.wait_ge(c.x_loaded, 16)

        @block.tensor
        def _(pe):
            pe.wait_ge(c.const_ready, 2)


def normalize(c, layer, scale=None, shift=None, given=None, twice=False, rms=False, loads=(), owed=None):
    nc = c.nc
    with ExitStack() as ctx:
        def sb(name, shape, dt=F32):
            return ctx.enter_context(nc.sbuf_tensor(f"{layer}_{name}", shape, dt))

        def sem(name):
            return c.layer_sem(f"{layer}_{name}")

        again = twice or rms
        rounds = 2 if again else 1
        stats = sb("stats", [P, B, 6])
        mv = sb("mv", [P, B, 2])
        ms = sb("ms", [P, B])
        root = sb("root", [P, B])
        rstd = sb("rstd", [P, B])
        a2 = sb("a2", [P, B, D]) if again else c.a
        n_cols = (scale is not None) + (shift is not None) if given is None else 2
        xt = sb("xt", [P, KC, T]) if n_cols else None
        warm = sb("warm", [P, 1])
        var_ready, root_ready, a_ready = sem("var_ready"), sem("root_ready"), sem("a_ready")
        t_ready, xt_ready, xt_hi_ready = sem("t_ready"), sem("xt_ready"), sem("xt_hi_ready")
        col, cols = given if given is not None else (sb("col", [P, 2, KC]), sem("cols"))

        def part(t, b):
            return t[:, :, b * P:(b + 1) * P]

        def turned(b):
            return c.psum[:, b, :].rearrange("p (k t) -> p k t", k=KC)

        with nc.Block(no_gpsimd_drain=True) as block:

            @block.sync
            def _(sp):
                for n, v in enumerate((scale, shift)):
                    if v is not None:
                        sp.dma_start(col[:, n, :], v).then_inc(cols, 16)
                for to, src, ready in loads:
                    sp.dma_start(to, src).then_inc(ready, 16)

            @block.vector
            def _(dve):
                own = c.dve_chain
                for rnd in range(rounds):
                    src, dst = ((c.x, c.a), (c.a, a2))[rnd]
                    for b in range(B):
                        own.done(dve.bn_stats(stats[:, b, :], src[:, b, :]))
                    own.wait()
                    for b in range(B):
                        own.done(dve.bn_aggr(mv[:, b, :], stats[:, b, :]))
                    own.wait()
                    if rnd and rms:
                        own.step(dve.tensor_tensor(ms[:], mv[:, :, 0], mv[:, :, 0], ALU.mult))
                        own.step(dve.tensor_tensor(ms[:], ms[:], mv[:, :, 1], ALU.add))
                    dve.sem_inc(var_ready, 1)
                    dve.wait_ge(root_ready, rnd + 1)
                    own.step(dve.reciprocal(rstd[:], root[:]))
                    for b in range(B):
                        if rnd and rms:
                            op = dve.tensor_scalar(dst[:, b, :], src[:, b, :], rstd[:, b:b + 1], None, ALU.mult)
                        else:
                            op = dve.tensor_scalar(dst[:, b, :], src[:, b, :], mv[:, b, 0:1], rstd[:, b:b + 1],
                                                   ALU.subtract, ALU.mult)
                        if rnd == rounds - 1:
                            op.then_inc(a_ready, 1)
                        else:
                            own.done(op)
                    own.wait()
                dve.wait_ge(a_ready, B)
                if owed is not None:
                    c.split_lo(dve, owed)
                if not n_cols:
                    for b in range(B):
                        dve.wait_ge(xt_hi_ready, b + 1)
                        own.done(dve.tensor_tensor(part(c.xt_lo, b), turned(b), part(c.xt_hi, b).bitcast(F32), ALU.subtract))
                    own.wait()
                    return
                dve.wait_ge(cols, 16 * n_cols)
                for b in range(B):
                    dve.wait_ge(t_ready, b + 1)
                    for k in range(KC):
                        src = c.psum[:, b, k * P:(k + 1) * P]
                        dst = xt[:, k, b * P:(b + 1) * P]
                        own.done(dve.tensor_scalar(dst, src, col[:, 0, k:k + 1],
                                                   col[:, 1, k:k + 1] if n_cols == 2 else 0.0, ALU.mult, ALU.add))
                    own.wait()
                    dve.sem_inc(xt_ready, 1)
                for b in range(B):
                    dve.wait_ge(xt_hi_ready, b + 1)
                    own.done(dve.tensor_tensor(part(c.xt_lo, b), part(xt, b), part(c.xt_hi, b).bitcast(F32), ALU.subtract))
                own.wait()

            @block.scalar
            def _(act):
                act.activation(warm[:], c.eps[:, 0:1], ACT.Sqrt)
                for rnd in range(rounds):
                    act.wait_ge(var_ready, rnd + 1)
                    act.activation(root[:], ms[:] if rnd and rms else mv[:, :, 1], ACT.Sqrt, bias=c.eps[:, 0:1]).then_inc(root_ready, 1)
                if not n_cols:
                    for b in range(B):
                        act.wait_ge(t_ready, b + 1)
                        act.copy(part(c.xt_hi, b), turned(b)).then_inc(xt_hi_ready, 1)
                    act.wait_ge(xt_hi_ready, B)
                    return
                for b in range(B):
                    act.wait_ge(xt_ready, b + 1)
                    act.copy(part(c.xt_hi, b), part(xt, b)).then_inc(xt_hi_ready, 1)
                act.wait_ge(xt_hi_ready, B)

            @block.tensor
            def _(pe):
                for b in range(B):
                    pe.wait_ge(a_ready, b + 1)
                    for k in range(KC):
                        t = pe.transpose(c.psum[:, b, k * P:(k + 1) * P], a2[:, b, k * P:(k + 1) * P], c.ident[:])
                    t.then_inc(t_ready, 1)
def turn_outputs(c, layer, o, ot_hi, ot_lo):
    nc = c.nc
    groups = o.shape[2] // 512

    def sem(name):
        return c.layer_sem(f"{layer}_{name}")

    turned, turned_hi, turned_lo = sem("turned"), sem("turned_hi"), sem("turned_lo")
    with nc.Block(no_gpsimd_drain=True) as block:

        @block.tensor
        def _(pe):
            for g in range(groups):
                for b in range(B):
                    for i in range(4):
                        k = 4 * g + i
                        t = pe.transpose(c.psum[:, 2 * g + b, i * P:(i + 1) * P], o[:, b, k * P:(k + 1) * P], c.ident[:])
                    t.then_inc(turned, 1)

        @block.scalar
        def _(act):
            for g in range(groups):
                for b in range(B):
                    act.wait_ge(turned, 2 * g + b + 1)
                    act.copy(ot_hi[:, 4 * g:4 * g + 4, b * P:(b + 1) * P],
                             c.psum[:, 2 * g + b, :].rearrange("p (k t) -> p k t", k=4)).then_inc(turned_hi, 1)

        @block.vector
        def _(dve):
            for g in range(groups):
                for b in range(B):
                    dve.wait_ge(turned_hi, 2 * g + b + 1)
                    dve.tensor_tensor(ot_lo[:, 4 * g:4 * g + 4, b * P:(b + 1) * P],
                                      c.psum[:, 2 * g + b, :].rearrange("p (k t) -> p k t", k=4),
                                      ot_hi[:, 4 * g:4 * g + 4, b * P:(b + 1) * P].bitcast(F32), ALU.subtract)\
                       .then_inc(turned_lo, 1)
            dve.wait_ge(turned_lo, 2 * groups)


def project_out(c, layer, ot_hi, ot_lo, first, tiles, bias=None):
    nc = c.nc

    with ExitStack() as ctx:
        if bias is not None:
            y = ctx.enter_context(nc.sbuf_tensor(f"{layer}_y", [P, B, D], F32))
        out_ready = c.layer_sem(f"{layer}_out_ready")
        with nc.Block(no_gpsimd_drain=True) as block:

            @block.sync
            def _(sp):
                for t in range(first + RAW, min(first + tiles + RAW, TILES)):
                    c.load_weight(sp, t)

            @block.scalar
            def _(act):
                for t in range(first + SPLIT, first + tiles + SPLIT):
                    c.split_hi(act, t)

            @block.tensor
            def _(pe):
                for t in range(tiles):
                    s = c.slot(first + t)
                    pe.wait_ge(c.lo_ready, first + t + 1)
                    for b in range(B):
                        for k in range(KC):
                            cols = slice(b * P, (b + 1) * P)
                            mm = three_passes(pe, c.psum[:, b, :], (ot_hi[:, KC * t + k, cols], ot_lo[:, KC * t + k, cols]),
                                              (c.w_hi[:, s, k, :], c.w_lo[:, s, k, :]),
                                              t == k == 0, t == tiles - 1 and k == KC - 1)
                        if t == tiles - 1 and b == 0:
                            mm.then_inc(out_ready, 1)
                    mm.then_inc(c.w_used, 1)

            @block.vector
            def _(dve):
                own = c.dve_chain
                if bias is not None:
                    own.done(dve.tensor_tensor(c.x[:], c.x[:], c.a[:], ALU.add))
                for t in range(first + SPLIT, first + tiles + SPLIT - 1):
                    c.split_lo(dve, t)
                own.wait()
                for b in range(B):
                    if b == 0:
                        dve.wait_ge(out_ready, 1)
                    else:
                        c.wait_products(dve, first + tiles - 1)
                    y_b = c.psum[:, b, :]
                    if bias is not None:
                        own.step(dve.tensor_tensor(y[:, b, :], y_b, bias[:], ALU.add))
                        own.step(dve.scalar_tensor_tensor(y[:, b, :], y[:, b, :], 0.01, y[:, b, :], ALU.mult, ALU.max))
                        y_b = y[:, b, :]
                    own.done(dve.tensor_tensor(c.x[:, b, :], c.x[:, b, :], y_b, ALU.add))
                own.wait()


def cross_attention_0(c, early, glance):
    nc = c.nc
    H, DH, PAIRS = 16, 64, 8
    CHUNKS = B * S // P
    N = 2
    GROUPS = ((0, 6), (6, 11), (11, 16))
    LO, HI = float(2.718281828459045 ** -11.0), float(2.718281828459045 ** 11.0)
    BT, BK, BV, BKT, BS, BO = 0, 1, 3, 4, 5, 7

    with ExitStack() as ctx:
        def sb(name, shape, dt=F32):
            return ctx.enter_context(nc.sbuf_tensor(f"x0_{name}", shape, dt))

        def sem(name):
            return c.layer_sem(f"x0_{name}")

        wk_lo = sb("wk_lo", [P, 2, KC, D], F32R)
        q_hi = sb("q_hi", [P, B, PAIRS, 2 * P], F32R)
        q_lo = sb("q_lo", [P, B, PAIRS, 2 * P], F32R)
        acc = sb("acc", [P, B, H, DH + 1])
        cos = sb("cos", [P, S // P, 32])
        sin = sb("sin", [P, S // P, 2, 32])
        col = sb("col", [P, 2, KC])
        mv = sb("mv", [P, B, S // P, 2])
        rstd = sb("rstd", [P, B, S // P])
        raw = sb("raw", [P, N, D])
        chunk_of = c.dram["ctx"].rearrange("b (j p) d -> b j p d", p=P)
        ctx_ready = [sem(f"ctx_ready{i}") for i in range(N)]

        q_ready, q_hi_ready, q_free = sem("q_ready"), sem("q_hi_ready"), sem("q_free")
        tables, zeroed = sem("tables"), sem("zeroed")

        G = GLANCE
        with (nc.sbuf_tensor("x0_stats", [P, B, G, 6], F32) as stats,
              nc.Block(no_gpsimd_drain=True) as block):
            stats_ready, mv_ready, root_ready = sem("stats_ready"), sem("mv_ready"), sem("root_ready")

            @block.sync
            def _(sp):
                sp.dma_start(cos[:], c.dram["cos"].rearrange("(j p) d -> p j d", p=P)).then_inc(tables, 16)
                sp.dma_start(sin[:, :, 0, :], c.dram["sin"].rearrange("(j p) d -> p j d", p=P)).then_inc(tables, 16)
                sp.dma_start(col[:, 0, :], c.dram["ln_ctx_g"]).then_inc(tables, 16)
                sp.dma_start(col[:, 1, :], c.dram["ln_ctx_b"]).then_inc(tables, 16)
                for g in range(1, S // P // G):
                    for b in range(B):
                        sp.wait_ge(stats_ready, B * g - B + b + 1)
                        sp.dma_start(glance[:, b], c.context_loads[b, g]).then_inc(c.seen[b], 16)
                for u in range(N):
                    sp.dma_start(raw[:, u, :], chunk_of[u, 0]).then_inc(ctx_ready[u], 16)
                for t in range(X0_WV, X0_WO):
                    c.load_weight(sp, t)

            @block.gpsimd
            def _(pool):
                pool.memset(q_hi[:].bitcast(F32), 0.0).then_inc(zeroed, 1)
                pool.memset(q_lo[:].bitcast(F32), 0.0).then_inc(zeroed, 1)
                pool.memset(acc[:], 0.0).then_inc(zeroed, 1)

            @block.scalar
            def _(act):
                for t in range(2):
                    c.split_hi(act, X0_WQ + t)
                act.wait_ge(zeroed, 3)
                for p in range(PAIRS):
                    act.wait_ge(q_ready, p + 1)
                    if p % 4 == 3:
                        act.sem_inc(c.w_used, 1)
                    for half in range(2):
                        r = slice(64 * half, 64 * half + 64)
                        act.copy(q_hi[r, :, p, P * half:P * half + P],
                                 c.psum[r, p % 4, 0:T].rearrange("p (b t) -> p b t", b=B)).then_inc(q_hi_ready, 1)
                act.wait_ge(mv_ready, B * S // P)
                act.activation(rstd[:], mv[:, :, :, 1], ACT.Sqrt, bias=c.eps[:, 0:1]).then_inc(root_ready, 1)

            @block.vector
            def _(dve):
                own = c.dve_chain

                def spreads(n):
                    g, b = divmod(n, B)
                    dve.wait_ge(c.seen[b], 16 * g + 16)
                    for i in range(G):
                        own.done(dve.bn_stats(stats[:, b, i], glance[:, b, i]))
                    own.wait()
                    dve.sem_inc(stats_ready, 1)
                    for i in range(G):
                        dve.bn_aggr(mv[:, b, G * g + i], stats[:, b, i]).then_inc(mv_ready, 1)
                    dve.wait_ge(mv_ready, G * (n + 1))

                spreads(0)
                for t in range(2):
                    c.split_lo(dve, X0_WQ + t)
                spreads(1)
                dve.wait_ge(zeroed, 3)
                for p in range(PAIRS):
                    for half in range(2):
                        r = slice(64 * half, 64 * half + 64)
                        dve.wait_ge(q_hi_ready, 2 * p + 2)
                        dst = q_lo[r, :, p, P * half:P * half + P]
                        dve.tensor_tensor(dst, c.psum[r, p % 4, 0:T].rearrange("p (b t) -> p b t", b=B),
                                          q_hi[r, :, p, P * half:P * half + P].bitcast(F32), ALU.subtract)\
                           .then_inc(q_free, 1)
                    if p + 2 < PAIRS:
                        spreads(p + 2)
                dve.wait_ge(root_ready, 1)
                own.step(dve.reciprocal(rstd[:], rstd[:]))
                dve.wait_ge(tables, 64)
                own.step(dve.tensor_scalar(sin[:, :, 1, :], sin[:, :, 0, :], -1.0, None, ALU.mult))

            @block.tensor
            def _(pe):
                for p in range(PAIRS):
                    t = X0_WQ + p // 4
                    if p % 4 == 0:
                        pe.wait_ge(c.lo_ready, t + 1)
                    if p >= 4:
                        pe.wait_ge(q_free, 2 * (p - 3))
                    for k in range(KC):
                        w = slice((p % 4) * P, (p % 4 + 1) * P)
                        mm = three_passes(pe, c.psum[:, p % 4, 0:T],
                                          (c.w_hi[:, t % 2, k, w], c.w_lo[:, t % 2, k, w]),
                                          (c.xt_hi[:, k, :], c.xt_lo[:, k, :]), k == 0, k == KC - 1)
                    mm.then_inc(q_ready, 1)

        early.close()
        with ExitStack() as ctx:
            wk_hi = ctx.enter_context(nc.sbuf_tensor("x0_wk_hi", [P, RESIDENT, KC, D], F32R, side="right"))
            ct = sb("ct", [P, KC, P])
            ct_hi = sb("ct_hi", [P, N, KC, P], F32R)
            ct_lo = sb("ct_lo", [P, N, KC, P], F32R)
            kc = sb("kc", [P, 2 * D])
            ks = sb("ks", [P, 2 * D])
            kt_hi = sb("kt_hi", [P, PAIRS, P], F32R)
            kt_lo = sb("kt_lo", [P, PAIRS, P], F32R)
            v = sb("v", [P, N, H, DH + 1])
            pr = sb("pr", [P, H * P])
            own = c.dve_chain

            n_ready = sem("n_ready")
            t_ready, ct_ready, ct_hi_ready, ct_lo_ready = sem("t_ready"), sem("ct_ready"), sem("ct_hi_ready"), sem("ct_lo_ready")
            k_ready, k_read, k_rot, kt_ready = sem("k_ready"), sem("k_read"), sem("k_rot"), sem("kt_ready")
            kt_hi_ready, kt_lo_ready = sem("kt_hi_ready"), sem("kt_lo_ready")
            v_ready, v_out, s_ready, p_ready, p_clamped = sem("v_ready"), sem("v_out"), sem("s_ready"), sem("p_ready"), sem("p_clamped")
            o_ready, o_out, ones_ready = sem("o_ready"), sem("o_out"), sem("ones_ready")

            with nc.Block(no_gpsimd_drain=True) as block:

                @block.sync
                def _(sp):
                    def load(n, u, j):
                        if not isinstance(n, int) or n >= N:
                            sp.wait_ge(t_ready, n - (N - 1))
                        src = chunk_of[u, j] if isinstance(j, int) else chunk_of[u, bass.ds(j, 1)].rearrange("a p d -> (a p) d")
                        sp.dma_start(raw[:, u, :], src).then_inc(ctx_ready[u], 16)

                    for t in range(X0_WK + RAW, X0_WO + RAW):
                        c.load_weight(sp, t)
                    with sp.Fori(1, S // P) as j:
                        for u in range(2):
                            load(j * 2 + u, u, j)

                @block.gpsimd
                def _(pool):
                    pool.memset(v[:, :, :, DH:DH + 1], 1.0).then_inc(ones_ready, 1)

                    def rotate(n):
                        pool.wait_ge(k_read, n * 3 + 3)
                        pool.tensor_tensor(kc[:], kc[:], ks[:], ALU.add).then_inc(k_rot, 1)

                    rotate(0)
                    with pool.Fori(1, CHUNKS) as n:
                        rotate(n)

                @block.scalar
                def _(act):
                    act.wait_ge(ones_ready, 1)

                    def context_hi(n, u):
                        act.wait_ge(ct_ready, n + 1)
                        act.copy(ct_hi[:, u], ct[:]).then_inc(ct_hi_ready, 1)

                    def values(n, u, half):
                        act.wait_ge(v_ready, n * 2 + (half + 1))
                        act.copy(v[:, u, 8 * half:8 * half + 8, 0:DH],
                                 c.psum[:, BV, :].rearrange("p (h d) -> p h d", d=DH)).then_inc(v_out, 1)

                    def keys_hi(n, half):
                        act.wait_ge(kt_ready, n * 2 + (half + 1))
                        act.copy(kt_hi[:, 4 * half:4 * half + 4, :],
                                 c.psum[:, BKT, :].rearrange("p (h d) -> p h d", d=P)).then_inc(kt_hi_ready, 1)

                    def exps(n, quarter):
                        act.wait_ge(s_ready, n * 4 + (quarter + 1))
                        act.activation(pr[:, 512 * quarter:512 * quarter + 512], c.psum[:, BS + quarter % 2, :],
                                       ACT.Exp, scale=DH ** -0.5).then_inc(p_ready, 1)

                    def chunk(n, u, project=True, attend=True, ahead=True):
                        if attend:
                            keys_hi(n - 1, 0)
                            exps(n - 1, 0)
                            exps(n - 1, 1)
                            keys_hi(n - 1, 1)
                        if project:
                            values(n, u, 0)
                        if ahead:
                            context_hi(n + 1, 1 - u)
                        if attend:
                            exps(n - 1, 2)
                            exps(n - 1, 3)
                        if project:
                            values(n, u, 1)

                    c.split_hi(act, X0_WK, to=wk_hi[:, 0])
                    context_hi(0, 0)
                    c.split_hi(act, X0_WK + 1, to=wk_hi[:, 1])
                    for t in range(2):
                        c.split_hi(act, X0_WV + t)
                    chunk(0, 0, attend=False)
                    with act.Fori(0, CHUNKS // 2 - 1) as j:
                        chunk(j * 2 + 1, 1)
                        chunk(j * 2 + 2, 0)
                    chunk(CHUNKS - 1, 1, ahead=False)
                    act.sem_inc(c.w_used, 2)
                    for t in range(2):
                        c.split_hi(act, X0_WO + t)
                    chunk(CHUNKS, 0, project=False, ahead=False)

                @block.vector
                def _(dve):
                    dve.sem_inc(o_out, 1)

                    def norm(n, u, j):
                        dve.wait_ge(ctx_ready[u], j * 16 + 16)
                        at = slice(j, j + 1) if isinstance(j, int) else bass.ds(j, 1)
                        dve.tensor_scalar(raw[:, u, :], raw[:, u, :], mv[:, u, at, 0], rstd[:, u, at],
                                          ALU.subtract, ALU.mult).then_inc(n_ready, 1)

                    def context_out(n):
                        dve.wait_ge(t_ready, n + 1)
                        if not isinstance(n, int) or n >= 1:
                            dve.wait_ge(ct_lo_ready, n)
                        for k in range(KC):
                            own.done(dve.tensor_scalar(ct[:, k, :], c.psum[:, BT, k * P:(k + 1) * P],
                                                       col[:, 0, k:k + 1], col[:, 1, k:k + 1], ALU.mult, ALU.add))
                        own.wait()
                        dve.sem_inc(ct_ready, 1)

                    def context_lo(n, u):
                        dve.wait_ge(ct_hi_ready, n + 1)
                        dve.tensor_tensor(ct_lo[:, u], ct[:], ct_hi[:, u].bitcast(F32), ALU.subtract).then_inc(ct_lo_ready, 1)

                    def keys(n, j):
                        dve.wait_ge(k_ready, n * 2 + 2)
                        if not isinstance(n, int) or n >= 1:
                            dve.wait_ge(kt_ready, n * 2)
                        kp = c.psum[:, BK:BK + 2, :].rearrange("p b (h e d) -> p (b h) e d", e=2, d=32)
                        at = j if isinstance(j, int) else None
                        cs = cos[:, at:at + 1, :] if at is not None else cos[:, bass.ds(j, 1), :]
                        sn = sin[:, at:at + 1] if at is not None else sin[:, bass.ds(j, 1)]
                        sn = sn.rearrange("p a e d -> p (a e) d")
                        kcv = kc[:].rearrange("p (g d) -> p g d", d=32)
                        ksv = ks[:].rearrange("p (h e d) -> p h e d", e=2, d=32)
                        dve.tensor_tensor(kcv, kp.rearrange("p h e d -> p (h e) d"), cs.broadcast_to((P, 32, 32)), ALU.mult)\
                           .then_inc(k_read, 1)
                        for e in range(2):
                            dve.tensor_tensor(ksv[:, :, 1 - e, :], kp[:, :, e, :],
                                              sn[:, e:e + 1, :].broadcast_to((P, H, 32)), ALU.mult).then_inc(k_read, 1)

                    def keys_lo(n, half):
                        dve.wait_ge(kt_hi_ready, n * 2 + (half + 1))
                        dve.tensor_tensor(kt_lo[:, 4 * half:4 * half + 4, :],
                                          c.psum[:, BKT, :].rearrange("p (h d) -> p h d", d=P),
                                          kt_hi[:, 4 * half:4 * half + 4, :].bitcast(F32), ALU.subtract).then_inc(kt_lo_ready, 1)

                    def clamp(n, quarter):
                        dve.wait_ge(p_ready, n * 4 + (quarter + 1))
                        q = pr[:, 512 * quarter:512 * quarter + 512]
                        dve.tensor_scalar(q, q, LO, HI, ALU.max, ALU.min).then_inc(p_clamped, 1)

                    def gather_out(n, u, g):
                        a, b = GROUPS[g]
                        dve.wait_ge(o_ready, n * 3 + (g + 1))
                        w = acc[:, u, a:b, :].rearrange("p h d -> p (h d)")
                        dve.tensor_tensor(w, w, c.psum[:, BO, 0:(b - a) * (DH + 1)], ALU.add).then_inc(o_out, 1)

                    def chunk(n, u, j, project=True, score=True, output=True, ahead=True):
                        if output:
                            gather_out(n - 2, u, 0)
                        if score:
                            keys_lo(n - 1, 0)
                        if output:
                            gather_out(n - 2, u, 1)
                        if ahead:
                            norm(n + 1, 1 - u, j + u)
                        if score:
                            clamp(n - 1, 0)
                            clamp(n - 1, 1)
                            keys_lo(n - 1, 1)
                        if project:
                            keys(n, j)
                        if ahead:
                            context_out(n + 1)
                        if output:
                            gather_out(n - 2, u, 2)
                        if ahead:
                            context_lo(n + 1, 1 - u)
                        if score:
                            clamp(n - 1, 2)
                            clamp(n - 1, 3)

                    norm(0, 0, 0)
                    context_out(0)
                    c.split_lo(dve, X0_WK, to=wk_lo[:, 0], hi=wk_hi[:, 0])
                    context_lo(0, 0)
                    c.split_lo(dve, X0_WK + 1, to=wk_lo[:, 1], hi=wk_hi[:, 1])
                    for t in range(2):
                        c.split_lo(dve, X0_WV + t)
                    chunk(0, 0, 0, score=False, output=False)
                    chunk(1, 1, 0, output=False)
                    with dve.Fori(0, CHUNKS // 2 - 2) as j:
                        own.enter(j, 8)
                        chunk(j * 2 + 2, 0, j + 1)
                        chunk(j * 2 + 3, 1, j + 1)
                        own.leave(CHUNKS // 2 - 2)
                    chunk(CHUNKS - 2, 0, S // P - 1)
                    chunk(CHUNKS - 1, 1, S // P - 1, ahead=False)
                    chunk(CHUNKS, 0, S // P, project=False, ahead=False)
                    chunk(CHUNKS + 1, 1, S // P, project=False, score=False, ahead=False)
                    dve.wait_ge(o_out, CHUNKS * 3 + 1)
                    for t in range(2):
                        c.split_lo(dve, X0_WO + t)

                @block.tensor
                def _(pe):
                    def turn(n, u):
                        pe.wait_ge(n_ready, n + 1)
                        if not isinstance(n, int) or n >= 1:
                            pe.wait_ge(ct_ready, n)
                        for k in range(KC):
                            t = pe.transpose(c.psum[:, BT, k * P:(k + 1) * P], raw[:, u, k * P:(k + 1) * P], c.ident[:])
                        t.then_inc(t_ready, 1)

                    def project_k(n, u, half):
                        if isinstance(n, int) and n == 0:
                            pe.wait_ge(c.lo_ready, X0_WK + half + 1)
                        if half == 0:
                            pe.wait_ge(ct_lo_ready, n + 1)
                            if not isinstance(n, int) or n >= 1:
                                pe.wait_ge(k_read, n * 3)
                        for k in range(KC):
                            mm = three_passes(pe, c.psum[:, BK + half, :], (ct_hi[:, u, k, :], ct_lo[:, u, k, :]),
                                              (wk_hi[:, half, k, :], wk_lo[:, half, k, :]), k == 0, k == KC - 1)
                        mm.then_inc(k_ready, 1)

                    def project_v(n, u, half):
                        if not isinstance(n, int) or n * 2 + half >= 1:
                            pe.wait_ge(v_out, n * 2 + half)
                        if isinstance(n, int) and n == 0:
                            pe.wait_ge(c.lo_ready, X0_WV + half + 1)
                        for k in range(KC):
                            mm = three_passes(pe, c.psum[:, BV, :], (ct_hi[:, u, k, :], ct_lo[:, u, k, :]),
                                              (c.w_hi[:, half, k, :], c.w_lo[:, half, k, :]), k == 0, k == KC - 1)
                        mm.then_inc(v_ready, 1)

                    def turn_k(n, half):
                        if half == 0:
                            pe.wait_ge(k_rot, n + 1)
                        if not isinstance(n, int) or n * 2 + half >= 1:
                            pe.wait_ge(kt_lo_ready, n * 2 + half)
                        for i in range(4):
                            p = 4 * half + i
                            t = pe.transpose(c.psum[:, BKT, i * P:(i + 1) * P], kc[:, p * P:(p + 1) * P], c.ident[:])
                        t.then_inc(kt_ready, 1)

                    def scores(n, u, quarter):
                        if quarter % 2 == 0:
                            pe.wait_ge(kt_lo_ready, n * 2 + (quarter // 2 + 1))
                        if not isinstance(n, int) or n * 4 + quarter >= 2:
                            pe.wait_ge(p_ready, n * 4 + (quarter - 1))
                        for i in range(2):
                            p = 2 * quarter + i
                            mm = three_passes(pe, c.psum[:, BS + quarter % 2, 256 * i:256 * i + 256],
                                              (kt_hi[:, p, :], kt_lo[:, p, :]), (q_hi[:, u, p, :], q_lo[:, u, p, :]))
                        mm.then_inc(s_ready, 1)

                    def outputs(n, u, g):
                        a, b = GROUPS[g]
                        if g == 0:
                            pe.wait_ge(v_out, n * 2 + 2)
                            pe.wait_ge(p_clamped, n * 4 + 4)
                        pe.wait_ge(o_out, n * 3 + (g + 1))
                        for h in range(a, b):
                            mm = pe.matmul(c.psum[:, BO, (h - a) * (DH + 1):(h - a + 1) * (DH + 1)],
                                           pr[:, h * P:(h + 1) * P], v[:, u, h, :], start=True, stop=True)
                        mm.then_inc(o_ready, 1)

                    def chunk(n, u, project=True, score=True, output=True, ahead=True):
                        if project:
                            project_k(n, u, 0)
                        if output:
                            outputs(n - 2, u, 0)
                        if score:
                            turn_k(n - 1, 0)
                        if project:
                            project_k(n, u, 1)
                        if output:
                            outputs(n - 2, u, 1)
                        if score:
                            scores(n - 1, 1 - u, 0)
                            scores(n - 1, 1 - u, 1)
                            turn_k(n - 1, 1)
                        if project:
                            project_v(n, u, 0)
                        if ahead:
                            turn(n + 1, 1 - u)
                        if output:
                            outputs(n - 2, u, 2)
                        if score:
                            scores(n - 1, 1 - u, 2)
                            scores(n - 1, 1 - u, 3)
                        if project:
                            project_v(n, u, 1)

                    turn(0, 0)
                    chunk(0, 0, score=False, output=False)
                    chunk(1, 1, output=False)
                    with pe.Fori(0, CHUNKS // 2 - 2) as j:
                        chunk(j * 2 + 2, 0)
                        chunk(j * 2 + 3, 1)
                    chunk(CHUNKS - 2, 0)
                    chunk(CHUNKS - 1, 1, ahead=False)
                    chunk(CHUNKS, 0, project=False, ahead=False)
                    chunk(CHUNKS + 1, 1, project=False, score=False, ahead=False)

        with ExitStack() as ctx:
            o = sb("o", [P, B, H * DH])
            rsum = sb("rsum", [P, B, H])
            bias = sb("bias", [P, D])

            bias_ready, o_norm = sem("bias_ready"), sem("o_norm")
            with nc.Block(no_gpsimd_drain=True) as block:

                @block.sync
                def _(sp):
                    sp.dma_start(bias[:], c.dram["x0_bo"].partition_broadcast(P)).then_inc(bias_ready, 16)

                @block.vector
                def _(dve):
                    c.dve_chain.step(dve.reciprocal(rsum[:], acc[:, :, :, DH]))
                    for b in range(B):
                        dve.tensor_tensor(o[:, b, :].rearrange("p (h d) -> p h d", d=DH), acc[:, b, :, 0:DH],
                                          rsum[:, b, :].unsqueeze(2).broadcast_to((P, H, DH)), ALU.mult).then_inc(o_norm, 1)
                    dve.wait_ge(o_norm, 2)
                    dve.wait_ge(bias_ready, 16)
                    for b in range(B):
                        c.dve_chain.done(dve.tensor_tensor(c.x[:, b, :], c.x[:, b, :], bias[:], ALU.add))
                    c.dve_chain.wait()
            ot_hi = sb("ot_hi", [P, 8, T], F32R)
            ot_lo = sb("ot_lo", [P, 8, T], F32R)
            turn_outputs(c, "x0", o, ot_hi, ot_lo)
            project_out(c, "x0", ot_hi, ot_lo, X0_WO, 2)
def self_attention_0(c):
    nc = c.nc
    H, G, DV = 16, 4, 256
    SCALE = 32.0 ** -0.5
    VT = H * DV // D
    BV, BQ, BS = 0, 2, 4

    with ExitStack() as ctx:
        def sb(name, shape, dt=F32):
            return ctx.enter_context(nc.sbuf_tensor(f"a0_{name}", shape, dt))

        def sem(name):
            return c.layer_sem(f"a0_{name}")

        bias = sb("bias", [P, D])
        ot_hi = sb("ot_hi", [P, H * DV // P, T], F32R)
        ot_lo = sb("ot_lo", [P, H * DV // P, T], F32R)
        biases = sem("biases")
        with ExitStack() as ctx:
            bqk = sb("bqk", [P, 2 * KC])
            bv = sb("bv", [P, H * DV])
            qk = sb("qk", [P, 2, T])
            qk_sum = sb("qk_sum", [P, 2, T])
            q_hi = sb("q_hi", [P, G, T], F32R)
            q_lo = sb("q_lo", [P, G, T], F32R)
            k_hi, k_lo = (o[:, H * DV // P // 2:, :].rearrange("p a t -> p (a t)").rearrange(
                "p (b g n) -> p b g n", b=B, g=G) for o in (ot_hi, ot_lo))
            mx = sb("mx", [P, B * G, 4])
            total = sb("total", [P, B * G, 4])
            inv = sb("inv", [P, B * G, 4])
            v = sb("v", [P, 2, B, D])
            pr, pn = v[:, 0], v[:, 1]
            pt = sb("pt", [P, B, H, P])
            v_sum = sb("v_sum", [P, B, D])

            zeroed, qk_ready, qk_act, qk_hi, qk_lo = sem("zeroed"), sem("qk_ready"), sem("qk_act"), sem("qk_hi"), sem("qk_lo")
            s_ready, s_out, p_ready, inv_ready, pn_ready = sem("s_ready"), sem("s_out"), sem("p_ready"), sem("inv_ready"), sem("pn_ready")
            pt_ready, pt_out, v_read, v_act = sem("pt_ready"), sem("pt_out"), sem("v_read"), sem("v_act")
            o_ready, o_hi, o_lo = sem("o_ready"), sem("o_hi"), sem("o_lo")

            def score_bank(i):
                return BS + (i if i < 4 else i % 2)

            def value_bank(t):
                return BS + 2 if t == 1 else BV

            with nc.Block(no_gpsimd_drain=True) as block:

                @block.sync
                def _(sp):
                    sp.dma_start(bqk[:], c.dram["a0_bqk"]).then_inc(biases, 16)
                    sp.dma_start(bv[:], c.dram["a0_bv"].partition_broadcast(P)).then_inc(biases, 16)
                    sp.dma_start(bias[:], c.dram["a0_bo"].partition_broadcast(P)).then_inc(biases, 16)
                    for t in range(A0_WQK + RAW, A0_WO + RAW):
                        c.load_weight(sp, t)

                @block.gpsimd
                def _(pool):
                    pool.memset(k_hi.bitcast(F32), 0.0).then_inc(zeroed, 1)
                    pool.memset(k_lo.bitcast(F32), 0.0).then_inc(zeroed, 1)

                @block.scalar
                def _(act):
                    act.wait_ge(zeroed, 2)
                    for m in range(2 * G):
                        act.wait_ge(qk_act, m + 1)
                        if m < G:
                            act.copy(q_hi[:, m, :], qk[:, m % 2, :]).then_inc(qk_hi, 4)
                            continue
                        for h in range(4):
                            r = slice(32 * h, 32 * h + 32)
                            act.copy(k_hi[r, :, m - G, h * P:(h + 1) * P],
                                     qk[r, m % 2, :].rearrange("p (b t) -> p b t", b=B)).then_inc(qk_hi, 1)
                    c.split_hi(act, A0_WV)
                    c.split_hi(act, A0_WV + 1)

                    def probabilities(i):
                        act.wait_ge(inv_ready, i + 1)
                        if i >= 2:
                            act.wait_ge(pt_ready, i - 1)
                        for h in range(4):
                            cols = slice(h * P, (h + 1) * P)
                            act.activation(pn[:, i % 2, cols], pr[:, i % 2, cols], ACT.Copy, scale=inv[:, i, h:h + 1])\
                               .then_inc(pn_ready, 1)

                    for i in range(B * G):
                        act.wait_ge(s_out, i + 1)
                        act.activation(pr[:, i % 2, :], pr[:, i % 2, :], ACT.Exp, scale=SCALE).then_inc(p_ready, 1)
                        if i >= 1:
                            probabilities(i - 1)
                        if i >= 2:
                            act.wait_ge(pt_ready, i - 1)
                            act.copy(pt[:, (i - 2) // G, 4 * ((i - 2) % G):4 * ((i - 2) % G) + 4, :],
                                     c.psum[:, BQ + i % 2, :].rearrange("p (h t) -> p h t", h=4)).then_inc(pt_out, 1)
                    probabilities(B * G - 1)
                    for i in range(B * G - 2, B * G):
                        act.wait_ge(pt_ready, i + 1)
                        act.copy(pt[:, i // G, 4 * (i % G):4 * (i % G) + 4, :],
                                 c.psum[:, BQ + i % 2, :].rearrange("p (h t) -> p h t", h=4)).then_inc(pt_out, 1)

                    def high(t):
                        act.wait_ge(o_ready, t + 1)
                        bank = BS + 2 * (t % 2)
                        act.copy(ot_hi[:, 4 * t:4 * t + 4, :],
                                 c.psum[:, bank:bank + 2, :].rearrange("p a (k t) -> p (a k) t", k=2)).then_inc(o_hi, 1)

                    for t in range(VT):
                        c.split_hi(act, A0_WV + t + 2)
                        if t >= 1:
                            high(t - 1)
                    high(VT - 1)

                @block.vector
                def _(dve):
                    own = c.dve_chain
                    dve.wait_ge(zeroed, 2)
                    dve.wait_ge(biases, 48)

                    def lows(m):
                        dve.wait_ge(qk_hi, 4 * m + 4)
                        if m < G:
                            dve.tensor_tensor(q_lo[:, m, :], qk[:, m % 2, :], q_hi[:, m, :].bitcast(F32), ALU.subtract)\
                               .then_inc(qk_lo, 4)
                            return
                        for h in range(4):
                            r = slice(32 * h, 32 * h + 32)
                            dve.tensor_tensor(k_lo[r, :, m - G, h * P:(h + 1) * P],
                                              qk[r, m % 2, :].rearrange("p (b t) -> p b t", b=B),
                                              k_hi[r, :, m - G, h * P:(h + 1) * P].bitcast(F32), ALU.subtract).then_inc(qk_lo, 1)

                    for m in range(2 * G):
                        dve.wait_ge(qk_ready, m + 1)
                        if m % G == G - 1:
                            dve.sem_inc(c.w_used, 1)
                        if m >= 2:
                            dve.wait_ge(qk_lo, 4 * m - 4)
                        own.step(dve.tensor_scalar(qk_sum[:, m % 2, :], c.psum[:, BQ + m % 4, 0:T], bqk[:, m:m + 1], None, ALU.add))
                        dve.scalar_tensor_tensor(qk[:, m % 2, :], qk_sum[:, m % 2, :], 0.01, qk_sum[:, m % 2, :],
                                                 ALU.mult, ALU.max).then_inc(qk_act, 1)
                        if m >= 1:
                            lows(m - 1)
                    lows(2 * G - 1)
                    c.split_lo(dve, A0_WV)
                    c.split_lo(dve, A0_WV + 1)

                    def sums(i):
                        dve.wait_ge(p_ready, i + 1)
                        own.step(dve.tensor_reduce(total[:, i, :], pr[:, i % 2, :].rearrange("p (h k) -> p h k", h=4),
                                                   AX.X, ALU.add))
                        dve.reciprocal(inv[:, i, :], total[:, i, :]).then_inc(inv_ready, 1)

                    for i in range(B * G):
                        s = c.psum[:, score_bank(i), :].rearrange("p (h k) -> p h k", h=4)
                        dve.wait_ge(s_ready, i + 1)
                        if i >= 2:
                            dve.wait_ge(pn_ready, 4 * i - 4)
                        own.step(dve.tensor_reduce(mx[:, i, :], s, AX.X, ALU.max))
                        dve.tensor_tensor(pr[:, i % 2, :].rearrange("p (h k) -> p h k", h=4), s,
                                          mx[:, i, :].unsqueeze(2).broadcast_to((P, 4, P)), ALU.subtract).then_inc(s_out, 1)
                        if i >= 1:
                            sums(i - 1)
                    sums(B * G - 1)
                    dve.wait_ge(pt_ready, B * G)

                    def low(t):
                        dve.wait_ge(o_hi, t + 1)
                        bank = BS + 2 * (t % 2)
                        dve.tensor_tensor(ot_lo[:, 4 * t:4 * t + 4, :],
                                          c.psum[:, bank:bank + 2, :].rearrange("p a (k t) -> p (a k) t", k=2),
                                          ot_hi[:, 4 * t:4 * t + 4, :].bitcast(F32), ALU.subtract).then_inc(o_lo, 1)

                    for t in range(VT):
                        c.wait_products(dve, A0_WV + t)
                        if t >= 1:
                            dve.wait_ge(v_act, t)
                        if t >= 2:
                            dve.wait_ge(o_ready, t - 1)
                        for b in range(B):
                            dve.tensor_tensor(v_sum[:, b, :], c.psum[:, value_bank(t) + b, :], bv[:, D * t:D * t + D], ALU.add).then_inc(v_read, 1)
                        dve.wait_ge(v_read, 2 * t + 2)
                        dve.scalar_tensor_tensor(v[:, t % 2], v_sum[:], 0.01, v_sum[:], ALU.mult, ALU.max).then_inc(v_act, 1)
                        c.split_lo(dve, A0_WV + t + 2)
                        if t >= 1:
                            low(t - 1)
                    low(VT - 1)
                    dve.wait_ge(o_lo, VT)

                @block.tensor
                def _(pe):
                    for m in range(2 * G):
                        t = A0_WQK + m // G
                        if m % G == 0:
                            pe.wait_ge(c.lo_ready, t + 1)
                        if m >= 4:
                            pe.wait_ge(qk_act, m - 3)
                        w = slice((m % G) * P, (m % G + 1) * P)
                        for k in range(KC):
                            mm = three_passes(pe, c.psum[:, BQ + m % 4, 0:T],
                                              (c.w_hi[:, c.slot(t), k, w], c.w_lo[:, c.slot(t), k, w]),
                                              (c.xt_hi[:, k, :], c.xt_lo[:, k, :]), k == 0, k == KC - 1)
                        mm.then_inc(qk_ready, 1)
                    pe.wait_ge(qk_lo, 8 * G)

                    def scores(i):
                        b, g = divmod(i, G)
                        if i >= 4:
                            pe.wait_ge(s_out, i - 3 if i < 6 else i - 1)
                        cols = slice(b * P, (b + 1) * P)
                        three_passes(pe, c.psum[:, score_bank(i), :], (q_hi[:, g, cols], q_lo[:, g, cols]),
                                     (k_hi[:, b, g, :], k_lo[:, b, g, :])).then_inc(s_ready, 1)

                    def turn(i):
                        pe.wait_ge(pn_ready, 4 * i + 4)
                        if i >= 2:
                            pe.wait_ge(pt_out, i - 1)
                        for h in range(4):
                            x = pe.transpose(c.psum[:, BQ + i % 2, h * P:(h + 1) * P], pn[:, i % 2, h * P:(h + 1) * P], c.ident[:])
                        x.then_inc(pt_ready, 1)

                    def values(t, batch=range(B)):
                        pe.wait_ge(c.lo_ready, A0_WV + t + 1)
                        if t == 1:
                            pe.wait_ge(s_out, 4)
                        if t >= 2:
                            pe.wait_ge(v_read, 2 * t if t >= 3 else 2)
                        s = c.slot(A0_WV + t)
                        for b in batch:
                            cols = slice(b * P, (b + 1) * P)
                            for k in range(KC):
                                mm = three_passes(pe, c.psum[:, value_bank(t) + b, :], (c.xt_hi[:, k, cols], c.xt_lo[:, k, cols]),
                                                  (c.w_hi[:, s, k, :], c.w_lo[:, s, k, :]), k == 0, k == KC - 1)
                        if b == B - 1:
                            mm.then_inc(c.w_used, 1)

                    def outputs(t):
                        pe.wait_ge(v_act, t + 1)
                        if t >= 2:
                            pe.wait_ge(o_lo, t - 1)
                        for h in range(2):
                            for half in range(2):
                                for b in range(B):
                                    at = half * T + b * P
                                    mm = pe.matmul(c.psum[:, BS + 2 * (t % 2) + h, at:at + P],
                                                   v[:, t % 2, b, h * DV + half * P:h * DV + half * P + P],
                                                   pt[:, b, 2 * t + h, :], start=True, stop=True)
                        mm.then_inc(o_ready, 1)

                    for i in range(4):
                        scores(i)
                    values(0)
                    for i in range(2):
                        scores(4 + i)
                        turn(i)
                    for b in range(B):
                        turn(2 + b)
                        scores(6 + b)
                        values(1, (b,))
                    for i in range(4, 8):
                        turn(i)
                    pe.wait_ge(pt_out, B * G)
                    outputs(0)
                    for t in range(2, VT):
                        values(t)
                        outputs(t - 1)
                    outputs(VT - 1)

        project_out(c, "a0", ot_hi, ot_lo, A0_WO, VT, bias)


class GateInputs:

    def __init__(self, c, ctx, layer, bias=False):
        def sb(name, shape):
            return ctx.enter_context(c.nc.sbuf_tensor(f"{layer}_{name}", shape, F32))

        self.ready = c.layer_sem(f"{layer}_gate_ready")
        self.gw = sb("gw", [P, KC, E])
        self.b2 = sb("b2s", [E, D])
        self.loads = [(self.gw[:], c.dram[f"{layer}_gate_w"], self.ready), (self.b2[:], c.dram[f"{layer}_b2"], self.ready)]
        self.gb = None
        if bias:
            self.gb = sb("gb", [P, E])
            self.loads.append((self.gb[:], c.dram[f"{layer}_gate_b"].partition_broadcast(P), self.ready))


def gate(c, layer, gates, top, given, residual=False):
    nc = c.nc
    with ExitStack() as ctx:
        def sb(name, shape, dt=F32):
            return ctx.enter_context(nc.sbuf_tensor(f"{layer}_{name}", shape, dt))

        def sem(name):
            return c.layer_sem(f"{layer}_{name}")

        gw_hi = sb("gw_hi", [P, KC, E], F32R)
        gw_lo = sb("gw_lo", [P, KC, E], F32R)
        lane_i = sb("lane_i", [P, E], mybir.dt.int32)
        lane = sb("lane", [P, E])
        logit = sb("logit", [P, B, E])
        best = sb("best", [P, B, E])
        where = sb("where", [P, B, E], U32)
        wheref = sb("wheref", [P, B, E])
        less = sb("less", [P, B, E])
        ex = sb("ex", [P, B, E])
        total = sb("total", [P, B])
        prob = sb("prob", [P, B, 2])
        second = sb("second", [P, B, E])
        gt = sb("gt", [E, T])
        gw, gb, b2s = given.gw, given.gb, given.b2
        lanes, logits, shifted, ex_ready = sem("lanes"), sem("logits"), sem("shifted"), sem("ex_ready")
        gw_ready, g_ready, gt_ready, gt_out, y_ready = sem("gw_ready"), sem("g_ready"), sem("gt_ready"), sem("gt_out"), sem("gy_ready")

        with nc.Block(no_gpsimd_drain=True) as block:

            @block.gpsimd
            def _(pool):
                pool.iota(lane_i[:], pattern=[[1, E]], base=0, channel_multiplier=0).then_inc(lanes, 1)

            @block.scalar
            def _(act):
                act.wait_ge(shifted, 1)
                act.activation(ex[:], less[:], ACT.Exp).then_inc(ex_ready, 1)

            @block.vector
            def _(dve):
                own = c.dve_chain
                dve.wait_ge(given.ready, 16 * len(given.loads))
                own.step(dve.tensor_copy(gw_hi[:], gw[:]))
                dve.tensor_tensor(gw_lo[:], gw[:], gw_hi[:].bitcast(F32), ALU.subtract).then_inc(gw_ready, 1)
                dve.wait_ge(lanes, 1)
                own.step(dve.tensor_copy(lane[:], lane_i[:]))
                if residual:
                    own.step(dve.tensor_tensor(c.x[:], c.x[:], c.a[:], ALU.add))
                dve.wait_ge(logits, 1)
                for b in range(B):
                    if gb is not None:
                        own.step(dve.tensor_tensor(logit[:, b, :], c.psum[:, b, 0:E], gb[:], ALU.add))
                    else:
                        own.step(dve.tensor_copy(logit[:, b, :], c.psum[:, b, 0:E]))
                    own.step(dve.max(best[:, b, :], logit[:, b, :]))
                    own.step(dve.max_index(where[:, b, :], best[:, b, :], logit[:, b, :]))
                    own.step(dve.tensor_scalar(less[:, b, :], best[:, b, :] if top == 2 else logit[:, b, :],
                                               best[:, b, 0:1], None, ALU.subtract))
                dve.sem_inc(shifted, 1)
                own.step(dve.tensor_copy(wheref[:], where[:]))
                dve.wait_ge(ex_ready, 1)
                own.step(dve.tensor_reduce(total[:], ex[:, :, 0:top if top == 2 else E], AX.X, ALU.add))
                own.step(dve.reciprocal(prob[:, :, 0], total[:]))
                if top == 2:
                    own.step(dve.tensor_tensor(prob[:, :, 1], prob[:, :, 0], ex[:, :, 1], ALU.mult))
                for b in range(B):
                    own.step(dve.tensor_scalar(gates[:, b, :], lane[:], wheref[:, b, 0:1], prob[:, b, 0:1],
                                               ALU.is_equal, ALU.mult))
                    if top == 2:
                        own.step(dve.tensor_scalar(second[:, b, :], lane[:], wheref[:, b, 1:2], prob[:, b, 1:2],
                                                   ALU.is_equal, ALU.mult))
                        own.step(dve.tensor_tensor(gates[:, b, :], gates[:, b, :], second[:, b, :], ALU.add))
                dve.sem_inc(g_ready, 1)
                dve.wait_ge(gt_ready, 1)
                dve.tensor_copy(gt[:], c.psum[0:E, 2, 0:T]).then_inc(gt_out, 1)
                dve.wait_ge(y_ready, 1)
                own.step(dve.tensor_tensor(c.x[:], c.x[:], c.psum[:, 3:5, :], ALU.add))

            @block.tensor
            def _(pe):
                pe.wait_ge(gw_ready, 1)
                for b in range(B):
                    cols = slice(b * P, (b + 1) * P)
                    for k in range(KC):
                        mm = three_passes(pe, c.psum[:, b, 0:E], (c.xt_hi[:, k, cols], c.xt_lo[:, k, cols]),
                                          (gw_hi[:, k, :], gw_lo[:, k, :]), k == 0, k == KC - 1)
                mm.then_inc(logits, 1)
                pe.wait_ge(g_ready, 1)
                for b in range(B):
                    t = pe.transpose(c.psum[0:E, 2, b * P:(b + 1) * P], gates[:, b, :], c.ident[:])
                t.then_inc(gt_ready, 1)
                pe.wait_ge(gt_out, 1)
                for b in range(B):
                    mm = pe.matmul(c.psum[:, 3 + b, :], gt[:, b * P:(b + 1) * P], b2s[:], start=True, stop=True)
                mm.then_inc(y_ready, 1)


def experts_0(c, given):
    nc = c.nc
    W1, W2 = 4, 2
    PER = W1 + W2
    BH, BY = 0, 4
    LIMIT, ALPHA = 7.0, 1.702

    with ExitStack() as ctx:
        def sb(name, shape, dt=F32):
            return ctx.enter_context(nc.sbuf_tensor(f"f0_{name}", shape, dt))

        def sem(name):
            return c.layer_sem(f"f0_{name}")

        gates = sb("gates", [P, B, E])
        gate(c, "f0", gates, 2, given, residual=True)

        b1 = sb("b1", [P, E, 4 * W1])
        glu = sb("glu", [P, 2, 2, T])
        lin = sb("lin", [P, 2, 2, T])
        sig = sb("sig", [P, 2, 2, T])
        gated = sb("gated", [P, 2, 2, T])
        h = sb("h", [P, 2, 2, T])
        h_hi = sb("h_hi", [P, 2 * W1, T], F32R)
        h_lo = sb("h_lo", [P, 2 * W1, T], F32R)
        b1_ready, glu_ready, lin_ready, lin_ok = sem("b1_ready"), sem("glu_ready"), sem("lin_ready"), sem("lin_ok")
        sig_ready, gated_ready, h_ready, hi_ready, lo_ready = sem("sig_ready"), sem("gated_ready"), sem("h_ready"), sem("h_hi_ready"), sem("h_lo_ready")
        y_out = sem("ey_out")

        def expert(up, down, e, tile, i):
            up(e, 0, tile, i)
            down(e - 1, 0, tile + 1, i)
            up(e, 1, tile + 2, i)
            down(e - 1, 1, tile + 3, i)
            up(e, 2, tile + 4, i)
            up(e, 3, tile + 5, i)

        def before_loop(up, down):
            for t in range(W1):
                up(0, t, F0_W + t, 0)
            expert(up, down, 1, F0_W + W1, 0)

        def in_loop(up, down, j):
            for u in range(2):
                expert(up, down, j * 2 + (2 + u), F0_W + W1 + PER * (1 + u), j * (2 * PER))

        def after_loop(down):
            for t in range(W2):
                down(E - 1, t, F0_W + W1 + PER * (E - 1) + t, 0)

        with nc.Block(no_gpsimd_drain=True) as block:

            @block.sync
            def _(sp):
                sp.dma_start(b1[:], c.dram["f0_b1"]).then_inc(b1_ready, 16)
                with sp.Fori(0, PER * E // RAW) as j:
                    for n in range(RAW):
                        c.load_weight(sp, F0_W + RAW + n, j * RAW)

            @block.gpsimd
            def _(pool):
                with pool.Fori(0, W1 * E // 2) as j:
                    for q in range(2):
                        pool.wait_ge(sig_ready, j * 2 + (q + 1))
                        pool.tensor_tensor(gated[:, q], glu[:, q], sig[:, q], ALU.mult).then_inc(gated_ready, 1)

            @block.scalar
            def _(act):
                def high(s, t):
                    act.wait_ge(h_ready, s + 1)
                    act.copy(h_hi[:, 2 * t:2 * t + 2, :], h[:, t % 2]).then_inc(hi_ready, 1)

                def up(e, t, tile, i):
                    s, q = e * W1 + t, t % 2
                    c.wait_products(act, tile, i)
                    if t > 0 or not isinstance(e, int) or e > 0:
                        high(s - 1, (t - 1) % W1)
                    c.split_hi(act, tile + 2, i)
                    at = e if isinstance(e, int) else bass.ds(e, 1)
                    for x in range(2):
                        col = b1[:, at, 4 * t + 2 * x + 1:4 * t + 2 * x + 2]
                        act.activation(lin[:, q, x, :], c.psum[:, BH + 2 * q + 1, T * x:T * x + T], ACT.Identity, bias=col)\
                           .then_inc(lin_ready, 1)
                    act.wait_ge(glu_ready, s * 2 + 2)
                    act.activation(sig[:, q], glu[:, q], ACT.Sigmoid, scale=ALPHA).then_inc(sig_ready, 1)

                def down(e, t, tile, i):
                    c.split_hi(act, tile + 2, i)

                act.wait_ge(b1_ready, 16)
                before_loop(up, down)
                with act.Fori(0, (E - 2) // 2) as j:
                    in_loop(up, down, j)
                high(E * W1 - 1, W1 - 1)
                after_loop(down)

            @block.vector
            def _(dve):
                def low(s, t):
                    dve.wait_ge(hi_ready, s + 1)
                    dve.tensor_tensor(h_lo[:, 2 * t:2 * t + 2, :], h[:, t % 2], h_hi[:, 2 * t:2 * t + 2, :].bitcast(F32),
                                      ALU.subtract).then_inc(lo_ready, 1)

                def up(e, t, tile, i):
                    s, q = e * W1 + t, t % 2
                    c.wait_products(dve, tile, i)
                    at = e if isinstance(e, int) else bass.ds(e, 1)
                    for x in range(2):
                        col = b1[:, at, 4 * t + 2 * x:4 * t + 2 * x + 1]
                        dve.tensor_scalar(glu[:, q, x, :], c.psum[:, BH + 2 * q, T * x:T * x + T], col, LIMIT,
                                          ALU.add, ALU.min).then_inc(glu_ready, 1)
                    if t > 0 or not isinstance(e, int) or e > 0:
                        low(s - 1, (t - 1) % W1)
                    c.split_lo(dve, tile + 2, i)
                    dve.wait_ge(lin_ready, s * 2 + 2)
                    dve.tensor_scalar(lin[:, q], lin[:, q], LIMIT, -LIMIT, ALU.min, ALU.max).then_inc(lin_ok, 1)
                    dve.wait_ge(lin_ok, s + 1)
                    dve.wait_ge(gated_ready, s + 1)
                    dve.scalar_tensor_tensor(h[:, q], lin[:, q], 1.0, gated[:, q], ALU.add, ALU.mult).then_inc(h_ready, 1)

                def down(e, t, tile, i):
                    if t == W2 - 1:
                        c.wait_products(dve, tile, i)
                        at = slice(e, e + 1) if isinstance(e, int) else bass.ds(e, 1)
                        for b in range(B):
                            dve.scalar_tensor_tensor(c.x[:, b, :], c.psum[:, BY + b, :], gates[:, b, at], c.x[:, b, :],
                                                     ALU.mult, ALU.add).then_inc(y_out, 1)
                        dve.wait_ge(y_out, e * B + B)
                    c.split_lo(dve, tile + 2, i)

                dve.wait_ge(b1_ready, 16)
                before_loop(up, down)
                with dve.Fori(0, (E - 2) // 2) as j:
                    in_loop(up, down, j)
                low(E * W1 - 1, W1 - 1)
                after_loop(down)

            @block.tensor
            def _(pe):
                def up(e, t, tile, i):
                    s, slot = e * W1 + t, c.slot(tile)
                    pe.wait_ge(c.lo_ready, i + (tile + 1))
                    if not isinstance(e, int) or s >= 2:
                        pe.wait_ge(glu_ready, s * 2 - 2)
                        pe.wait_ge(lin_ready, s * 2 - 2)
                    for x in range(2 * 2):
                        w = slice(x * P, (x + 1) * P)
                        for k in range(KC):
                            mm = three_passes(pe, c.psum[:, BH + 2 * (t % 2) + x % 2, T * (x // 2):T * (x // 2) + T],
                                              (c.w_hi[:, slot, k, w], c.w_lo[:, slot, k, w]),
                                              (c.xt_hi[:, k, :], c.xt_lo[:, k, :]), k == 0, k == KC - 1)
                    mm.then_inc(c.w_used, 1)

                def down(e, t, tile, i):
                    slot = c.slot(tile)
                    pe.wait_ge(c.lo_ready, i + (tile + 1))
                    pe.wait_ge(lo_ready, e * W1 + (2 * t + 2))
                    if t == 0 and (not isinstance(e, int) or e > 0):
                        pe.wait_ge(y_out, e * B)
                    for b in range(B):
                        cols = slice(b * P, (b + 1) * P)
                        for k in range(KC):
                            mm = three_passes(pe, c.psum[:, BY + b, :], (h_hi[:, KC * t + k, cols], h_lo[:, KC * t + k, cols]),
                                              (c.w_hi[:, slot, k, :], c.w_lo[:, slot, k, :]),
                                              t == k == 0, t == W2 - 1 and k == KC - 1)
                    mm.then_inc(c.w_used, 1)

                before_loop(up, down)
                with pe.Fori(0, (E - 2) // 2) as j:
                    in_loop(up, down, j)
                after_loop(down)


def cross_attention_1(c):
    nc = c.nc
    H, G = 16, 4
    SCALE = 32.0 ** -0.5
    NB = 2
    BLOCKS = S // P // NB
    W = NB * P

    with ExitStack() as ctx:
        def sb(name, shape, dt=F32):
            return ctx.enter_context(nc.sbuf_tensor(f"x1_{name}", shape, dt))

        def sem(name):
            return c.layer_sem(f"x1_{name}")

        o = c.a
        q_hi, q_lo = c.xt_hi, c.xt_lo
        bq = sb("bq", [P, KC])
        bk = sb("bk", [P, KC])
        bv = sb("bv", [P, D])
        biases = sem("biases")
        raw = sb("raw", [P, 2, NB, D])
        some = c.dram["ctx"].rearrange("b (n u j p) d -> b n u p j d", p=P, j=NB, u=2)
        loaded = [[sem(f"loaded{b}{u}") for u in range(2)] for b in range(B)]

        with (nc.sbuf_tensor("x1_q", [P, G, T], F32) as q, nc.sbuf_tensor("x1_bias", [P, D], F32) as bias,
              nc.Block(no_gpsimd_drain=True) as block):
            q_ready, q_out, q_hi_ready, q_lo_ready = sem("q_ready"), sem("q_out"), sem("q_hi_ready"), sem("q_lo_ready")

            @block.sync
            def _(sp):
                for u in range(2):
                    sp.dma_start(raw[:, u], some[0, 0, u]).then_inc(loaded[0][u], 16)
                sp.dma_start(bq[:], c.dram["x1_bq"]).then_inc(biases, 16)
                sp.dma_start(bk[:], c.dram["x1_bk"]).then_inc(biases, 16)
                sp.dma_start(bv[:], c.dram["x1_bv"].partition_broadcast(P)).then_inc(biases, 16)
                sp.dma_start(bias[:], c.dram["x1_bo"].partition_broadcast(P)).then_inc(biases, 16)
                c.load_weight(sp, X1_WQ + RAW)

            @block.scalar
            def _(act):
                act.wait_ge(biases, 64)
                for g in range(G):
                    act.wait_ge(q_ready, g + 1)
                    act.activation(q[:, g, :], c.psum[:, g, 0:T], ACT.Identity, bias=bq[:, g:g + 1]).then_inc(q_out, 1)
                act.sem_inc(c.w_used, 1)
                act.wait_ge(q_out, G)
                act.copy(q_hi[:], q[:]).then_inc(q_hi_ready, 1)

            @block.vector
            def _(dve):
                dve.wait_ge(biases, 64)
                for b in range(B):
                    c.dve_chain.done(dve.tensor_tensor(c.x[:, b, :], c.x[:, b, :], bias[:], ALU.add))
                c.dve_chain.wait()
                dve.wait_ge(q_hi_ready, 1)
                dve.tensor_tensor(q_lo[:], q[:], q_hi[:].bitcast(F32), ALU.subtract).then_inc(q_lo_ready, 1)
                dve.wait_ge(q_lo_ready, 1)

            @block.tensor
            def _(pe):
                pe.wait_ge(c.lo_ready, X1_WQ + 1)
                for g in range(G):
                    w = slice(g * P, (g + 1) * P)
                    for k in range(KC):
                        s = c.slot(X1_WQ)
                        mm = three_passes(pe, c.psum[:, g, 0:T], (c.w_hi[:, s, k, w], c.w_lo[:, s, k, w]),
                                          (c.xt_hi[:, k, :], c.xt_lo[:, k, :]), k == 0, k == KC - 1)
                    mm.then_inc(q_ready, 1)

        with ExitStack() as ctx:
            kt_hi = sb("kt_hi", [P, G, S], F32R)
            kt_lo = sb("kt_lo", [P, G, S], F32R)
            v = sb("v", [P, S // P, D])
            for b in range(B):
                keys_values_1(c, b, raw, some[b], loaded[b], kt_hi, kt_lo, v, bk, W, NB, BLOCKS)
                attend_1(c, b, q_hi, q_lo, kt_hi, kt_lo, v, bv, o, SCALE,
                         [(raw[:, u], some[1, 0, u], loaded[1][u]) for u in range(2) if b == 0])

        turn_outputs(c, "x1", o, c.xt_hi, c.xt_lo)
        project_out(c, "x1", c.xt_hi, c.xt_lo, X1_WO, 1)


def keys_values_1(c, b, raw, some, loaded, kt_hi, kt_lo, v, bk, W, NB, BLOCKS):
    nc = c.nc
    G = KC
    BT, BK, BV = 0, 2, 6

    with ExitStack() as ctx:
        def sb(name, shape, dt=F32):
            return ctx.enter_context(nc.sbuf_tensor(f"kv{b}_{name}", shape, dt))

        def sem(name):
            return c.layer_sem(f"kv{b}_{name}")

        ct_hi = sb("ct_hi", [P, 2, KC, W], F32R)
        ct_lo = sb("ct_lo", [P, 2, KC, W], F32R)
        kf = sb("kf", [P, G, W])
        t_ready, ct_hi_ready, ct_lo_ready = sem("t_ready"), sem("ct_hi_ready"), sem("ct_lo_ready")
        k_ready, k_out, k_hi_ready, k_lo_ready = sem("k_ready"), sem("k_out"), sem("k_hi_ready"), sem("k_lo_ready")
        v_ready, v_out = sem("v_ready"), sem("v_out")

        with nc.Block(no_gpsimd_drain=True) as block:

            @block.sync
            def _(sp):
                if b == 0:
                    for t in range(X1_WK + RAW, X1_WV + RAW + 1):
                        c.load_weight(sp, t)
                with sp.Fori(1, BLOCKS // 2) as i:
                    for u in range(2):
                        sp.wait_ge(t_ready, NB * (i * 2 + u - 1))
                        sp.dma_start(raw[:, u], some[bass.ds(i, 1), u].rearrange("a p j d -> (a p) j d")).then_inc(loaded[u], 16)

            @block.scalar
            def _(act):
                def turned(n, u, first=False):
                    for j in range(NB):
                        act.wait_ge(t_ready, n * NB + (j + 1))
                        if j == 0 and not first:
                            act.wait_ge(v_ready, n * NB - NB)
                        act.copy(ct_hi[:, u, :, j * P:(j + 1) * P], c.psum[:, BT + j, :].rearrange("p (k t) -> p k t", k=KC))\
                           .then_inc(ct_hi_ready, 1)

                def block_of(n, u, ahead=True, first=False):
                    for g in range(G):
                        act.wait_ge(k_ready, n * G + (g + 1))
                        if g == 0 and not first:
                            act.wait_ge(k_lo_ready, n)
                        act.activation(kf[:, g, :], c.psum[:, BK + g, 0:W], ACT.Identity, bias=bk[:, g:g + 1]).then_inc(k_out, 1)
                    act.wait_ge(k_out, n * G + G)
                    at = slice(n * W, n * W + W) if isinstance(n, int) else bass.ds(n * W, W)
                    act.copy(kt_hi[:, :, at], kf[:]).then_inc(k_hi_ready, 1)
                    if ahead:
                        turned(n + 1, 1 - u, first)
                    for j in range(NB):
                        act.wait_ge(v_ready, n * NB + (j + 1))
                        to = v[:, n * NB + j, :] if isinstance(n, int) else v[:, bass.ds(n * NB + j, 1), :].rearrange("p a d -> p (a d)")
                        act.copy(to, c.psum[:, BV + j, :]).then_inc(v_out, 1)

                turned(0, 0, first=True)
                if b == 0:
                    c.split_hi(act, X1_WV)
                block_of(0, 0, first=True)
                with act.Fori(0, BLOCKS // 2 - 1) as i:
                    block_of(i * 2 + 1, 1)
                    block_of(i * 2 + 2, 0)
                block_of(BLOCKS - 1, 1, ahead=False)

            @block.vector
            def _(dve):
                def turned(n, u):
                    for j in range(NB):
                        dve.wait_ge(ct_hi_ready, n * NB + (j + 1))
                        cols = slice(j * P, (j + 1) * P)
                        dve.tensor_tensor(ct_lo[:, u, :, cols], c.psum[:, BT + j, :].rearrange("p (k t) -> p k t", k=KC),
                                          ct_hi[:, u, :, cols].bitcast(F32), ALU.subtract).then_inc(ct_lo_ready, 1)

                def block_of(n, u, ahead=True):
                    dve.wait_ge(k_hi_ready, n + 1)
                    at = slice(n * W, n * W + W) if isinstance(n, int) else bass.ds(n * W, W)
                    dve.tensor_tensor(kt_lo[:, :, at], kf[:], kt_hi[:, :, at].bitcast(F32), ALU.subtract).then_inc(k_lo_ready, 1)
                    if ahead:
                        turned(n + 1, 1 - u)

                turned(0, 0)
                if b == 0:
                    c.split_lo(dve, X1_WV)
                block_of(0, 0)
                with dve.Fori(0, BLOCKS // 2 - 1) as i:
                    block_of(i * 2 + 1, 1)
                    block_of(i * 2 + 2, 0)
                block_of(BLOCKS - 1, 1, ahead=False)
                dve.wait_ge(k_lo_ready, BLOCKS)
                if b == B - 1:
                    dve.wait_ge(v_ready, BLOCKS * NB)
                    dve.sem_inc(c.w_used, 2)

            @block.tensor
            def _(pe):
                sk, sv = c.slot(X1_WK), c.slot(X1_WV)

                def turn(n, u, i, first=False):
                    pe.wait_ge(loaded[u], i * 16 + 16)
                    if not first:
                        pe.wait_ge(ct_lo_ready, n * NB)
                    for j in range(NB):
                        for k in range(KC):
                            t = pe.transpose(c.psum[:, BT + j, k * P:(k + 1) * P], raw[:, u, j, k * P:(k + 1) * P], c.ident[:])
                        t.then_inc(t_ready, 1)

                def block_of(n, u, i, ahead=True, first=False):
                    if first:
                        pe.wait_ge(c.lo_ready, X1_WK + 1)
                    pe.wait_ge(ct_lo_ready, n * NB + NB)
                    if not first:
                        pe.wait_ge(k_out, n * G)
                    for g in range(G):
                        w = slice(g * P, (g + 1) * P)
                        for k in range(KC):
                            mm = three_passes(pe, c.psum[:, BK + g, 0:W], (c.w_hi[:, sk, k, w], c.w_lo[:, sk, k, w]),
                                              (ct_hi[:, u, k, :], ct_lo[:, u, k, :]), k == 0, k == KC - 1)
                        mm.then_inc(k_ready, 1)
                    if ahead:
                        turn(n + 1, 1 - u, i + u)
                    if first:
                        pe.wait_ge(c.lo_ready, X1_WV + 1)
                    else:
                        pe.wait_ge(v_out, n * NB)
                    for j in range(NB):
                        cols = slice(j * P, (j + 1) * P)
                        for k in range(KC):
                            mm = three_passes(pe, c.psum[:, BV + j, :], (ct_hi[:, u, k, cols], ct_lo[:, u, k, cols]),
                                              (c.w_hi[:, sv, k, :], c.w_lo[:, sv, k, :]), k == 0, k == KC - 1)
                        mm.then_inc(v_ready, 1)

                turn(0, 0, 0, first=True)
                block_of(0, 0, 0, first=True)
                with pe.Fori(0, BLOCKS // 2 - 1) as i:
                    block_of(i * 2 + 1, 1, i)
                    block_of(i * 2 + 2, 0, i + 1)
                block_of(BLOCKS - 1, 1, BLOCKS // 2 - 1, ahead=False)


def attend_1(c, b, q_hi, q_lo, kt_hi, kt_lo, v, bv, o, SCALE, next_loads):
    nc = c.nc
    HG, SC = 4, S // D
    HEADS = 16
    CH = S // P
    BS, BT, BO = 0, 4, 7

    with ExitStack() as ctx:
        def sb(name, shape, dt=F32):
            return ctx.enter_context(nc.sbuf_tensor(f"at{b}_{name}", shape, dt))

        def sem(name):
            return c.layer_sem(f"at{b}_{name}")

        qz_hi = sb("qz_hi", [P, HG, P], F32R)
        qz_lo = sb("qz_lo", [P, HG, P], F32R)
        pr = sb("pr", [P, S])
        pt = sb("pt", [P, CH, P])
        mx = sb("mx", [P, 2, SC])
        nmx = sb("nmx", [P, 2])
        part = sb("part", [P, 2, HG, SC])
        total = sb("total", [P, HG])
        inv = sb("inv", [P, HG])
        og = sb("og", [P, P])
        zeroed, qz_ready = sem("zeroed"), sem("qz_ready")
        s_ready, m_ready, p_ready, t_ready, pt_act, pt_dve = sem("s_ready"), sem("m_ready"), sem("p_ready"), sem("t_ready"), sem("pt_act"), sem("pt_dve")
        o_ready, o_out, g_ready, g_out = sem("o_ready"), sem("o_out"), sem("g_ready"), sem("g_out")

        with nc.Block(no_gpsimd_drain=True) as block:

            @block.sync
            def _(sp):
                for to, src, ready in next_loads:
                    sp.dma_start(to, src).then_inc(ready, 16)

            @block.gpsimd
            def _(pool):
                own = c.pool_chain
                own.done(pool.memset(qz_hi[:].bitcast(F32), 0.0))
                own.done(pool.memset(qz_lo[:].bitcast(F32), 0.0))
                own.wait()
                for n in range(HEADS):
                    g, h = divmod(n, HG)
                    r = slice(32 * h, 32 * h + 32)
                    if g >= 1:
                        pool.wait_ge(s_ready, (n - HG + 1) * SC)
                    for z, q in ((qz_hi, q_hi), (qz_lo, q_lo)):
                        pool.tensor_copy(z[r, h, :], q[r, g, b * P:(b + 1) * P].bitcast(F32)).then_inc(qz_ready, 1)

            @block.scalar
            def _(act):
                def exps(n):
                    g, h = divmod(n, HG)
                    act.wait_ge(m_ready, n + 1)
                    if h == 0 and g >= 2:
                        act.wait_ge(g_out, g - 1)
                    for i in range(SC):
                        act.activation(pr[:, i * D:(i + 1) * D], c.psum[:, BS + i, :], ACT.Exp, scale=SCALE,
                                       bias=nmx[:, n % 2:n % 2 + 1], accum_out=part[:, g % 2, h, i:i + 1]).then_inc(p_ready, 1)

                def turned(n):
                    for i in range(3):
                        act.wait_ge(t_ready, n * 4 + i + 1)
                        if i == 0 and n >= 1:
                            act.wait_ge(o_ready, n)
                        act.copy(pt[:, 4 * i:4 * i + 4, :], c.psum[:, BT + i, :].rearrange("p (j t) -> p j t", j=4)).then_inc(pt_act, 1)

                exps(0)
                for n in range(1, HEADS):
                    turned(n - 1)
                    exps(n)
                if b == B - 1:
                    for t in range(X1_WO, X1_WO + SPLIT):
                        c.split_hi(act, t)
                turned(HEADS - 1)

            @block.vector
            def _(dve):
                own = c.dve_chain

                def maximum(n):
                    for i in range(SC):
                        dve.wait_ge(s_ready, n * SC + i + 1)
                        own.done(dve.tensor_reduce(mx[:, n % 2, i:i + 1], c.psum[:, BS + i, :], AX.X, ALU.max))
                    own.wait()
                    own.step(dve.tensor_reduce(mx[:, n % 2, 0:1], mx[:, n % 2, :], AX.X, ALU.max))
                    dve.tensor_scalar(nmx[:, n % 2:n % 2 + 1], mx[:, n % 2, 0:1], -SCALE, None, ALU.mult).then_inc(m_ready, 1)

                def turned(n):
                    dve.wait_ge(t_ready, n * 4 + 4)
                    dve.wait_ge(pt_act, n * 3 + 1)
                    dve.tensor_copy(pt[:, 12:16, :], c.psum[:, BT, :].rearrange("p (j t) -> p j t", j=4)).then_inc(pt_dve, 1)

                def output(n):
                    h = n % HG
                    r = slice(32 * h, 32 * h + 32)
                    dve.wait_ge(o_ready, n + 1)
                    dve.tensor_copy(og[r, :], c.psum[r, BO, 0:P]).then_inc(o_out, 1)

                def group(g):
                    dve.wait_ge(p_ready, (g + 1) * HG * SC)
                    own.step(dve.tensor_reduce(total[:], part[:, g % 2], AX.X, ALU.add))
                    own.step(dve.reciprocal(inv[:], total[:]))
                    dve.wait_ge(g_ready, g + 1)
                    dve.tensor_tensor(o[:, b, g * P:(g + 1) * P].rearrange("p (h d) -> p h d", h=HG),
                                      c.psum[:, BO, 0:P].rearrange("p (h d) -> p h d", h=HG),
                                      inv[:].unsqueeze(2).broadcast_to((P, HG, 32)), ALU.mult).then_inc(g_out, 1)
                    dve.wait_ge(g_out, g + 1)

                maximum(0)
                for n in range(1, HEADS):
                    turned(n - 1)
                    if n % HG == 1 and n > 1:
                        group(n // HG - 1)
                    maximum(n)
                    output(n - 1)
                if b == B - 1:
                    for t in range(X1_WO, X1_WO + SPLIT):
                        c.split_lo(dve, t)
                turned(HEADS - 1)
                output(HEADS - 1)
                group(HEADS // HG - 1)
                own.step(dve.tensor_tensor(o[:, b, :], o[:, b, :], bv[:], ALU.add))

            @block.tensor
            def _(pe):
                def scores(n):
                    g, h = divmod(n, HG)
                    pe.wait_ge(qz_ready, n * 2 + 2)
                    for i in range(SC):
                        if n >= 1:
                            pe.wait_ge(p_ready, (n - 1) * SC + i + 1)
                        cols = slice(i * D, (i + 1) * D)
                        three_passes(pe, c.psum[:, BS + i, :], (qz_hi[:, h, :], qz_lo[:, h, :]),
                                     (kt_hi[:, g, cols], kt_lo[:, g, cols])).then_inc(s_ready, 1)

                def turn(n):
                    for i in range(4):
                        pe.wait_ge(p_ready, n * SC + i + 1)
                        if i == 3:
                            pe.wait_ge(pt_act, n * 3 + 1)
                        elif n >= 1:
                            pe.wait_ge(pt_dve, n)
                        for j in range(4):
                            t = pe.transpose(c.psum[:, BT + i % 3, j * P:(j + 1) * P], pr[:, (4 * i + j) * P:(4 * i + j + 1) * P],
                                             c.ident[:])
                        t.then_inc(t_ready, 1)

                def turn_group(g):
                    pe.wait_ge(o_out, (g + 1) * HG)
                    pe.transpose(c.psum[:, BO, 0:P], og[:], c.ident[:]).then_inc(g_ready, 1)

                def outputs(n):
                    g, h = divmod(n, HG)
                    if h == 0 and g >= 1:
                        pe.wait_ge(g_out, g)
                    pe.wait_ge(pt_act, n * 3 + 3)
                    pe.wait_ge(pt_dve, n + 1)
                    if n >= 1:
                        pe.wait_ge(o_out, n)
                    for j in range(CH):
                        mm = pe.matmul(c.psum[:, BO, 0:P], v[:, j, g * P:(g + 1) * P], pt[:, j, :], start=(j == 0), stop=(j == CH - 1))
                    mm.then_inc(o_ready, 1)

                scores(0)
                for n in range(1, HEADS):
                    turn(n - 1)
                    if n % HG == 1 and n > 1:
                        turn_group(n // HG - 1)
                    scores(n)
                    outputs(n - 1)
                turn(HEADS - 1)
                outputs(HEADS - 1)
                turn_group(HEADS // HG - 1)


def linear_attention_1(c):
    nc = c.nc
    HD = 64
    WT = HD * HD // D
    PASS = 4
    TU = 512 // HD
    UNITS = P // TU
    CB = 512 // P
    BK, BQ, BV, BN, BO, BY = 0, 4, 0, 4, 0, 6
    SUMS_AT, SPREAD_AT = 2, WT - 2

    with ExitStack() as ctx:
        def sb(name, shape, dt=F32):
            return ctx.enter_context(nc.sbuf_tensor(f"a1_{name}", shape, dt))

        def sem(name):
            return c.layer_sem(f"a1_{name}")

        v = sb("v", [P, P, P])
        q = sb("q", [P, P, HD])
        out = q[:].rearrange("p t i -> p (t i)").rearrange("p (u c b t) -> p u c b t", u=UNITS, c=HD // 2, b=B)
        ot_hi = sb("ot_hi", [P, 2, KC, B, P], F32R)
        ot_lo = sb("ot_lo", [P, 2, KC, B, P], F32R)
        ones = sb("ones", [P, B])
        inv = sb("inv", [P, UNITS * CB, B])
        ksum = sb("ksum", [P, B, P])
        shift = sb("shift", [P, T])
        tiny = sb("tiny", [P, 1])
        bias = sb("bias", [P, D])
        k_acc = c.a
        wide = c.a
        bias_ready, zeroed = sem("bias_ready"), sem("zeroed")
        k_ready, k_free, q_ready, q_free = sem("k_ready"), sem("k_free"), sem("q_ready"), sem("q_free")
        v_ready, v_act, v_dve = sem("v_ready"), sem("v_act"), sem("v_dve")
        summed, norm_out, inv_ready = sem("summed"), sem("norm_out"), sem("inv_ready")
        widened, spread, divided = sem("widened"), sem("spread"), sem("divided")
        o_ready, o_act, o_dve = sem("o_ready"), sem("o_act"), sem("o_dve")
        ot_hi_ready, ot_lo_ready, y_out = sem("ot_hi_ready"), sem("ot_lo_ready"), sem("y_out")

        def half_of(x):
            return slice(HD * x, HD * x + HD)

        def unit(u):
            return slice(TU * u, TU * u + TU)

        def chunks_of(bank):
            return c.psum[:, bank, :].rearrange("p (c b t) -> p b t c", c=2, b=B)

        def v_quadrants(bank, pair):
            return [(v[half_of(b), :, b * HD:(b + 1) * HD].rearrange("p t (g c e) -> p t g c e", c=2, e=2)[:, :, pair, :, e],
                     chunks_of(bank)[half_of(e), b]) for b in range(B) for e in range(2)]

        def out_quadrants(u):
            src = c.psum[:, BO + u % 4, :].rearrange("p (t c e) -> p c t e", t=TU, e=2)
            return [(out[half_of(e), u, :, b, :], src[half_of(b), :, :, e]) for b in range(B) for e in range(2)]

        def of_tile(n, b):
            return out[:, :, KC * n:KC * n + KC, b, :].rearrange("p u c t -> p c u t")

        def part(ot, n, b):
            return ot[:, n % 2, :, b, :].rearrange("p c (u t) -> p c u t", u=UNITS)

        with nc.Block(no_gpsimd_drain=True) as block:

            @block.sync
            def _(sp):
                sp.dma_start(bias[:], c.dram["a1_bo"].partition_broadcast(P)).then_inc(bias_ready, 16)
                with sp.Fori(0, 4 * WT // RAW) as i:
                    for n in range(RAW):
                        c.load_weight(sp, A1_WK + RAW + n, i * RAW)

            @block.gpsimd
            def _(pool):
                own = c.pool_chain
                pool.memset(tiny[:], 1e-6).then_inc(zeroed, 1)
                own.step(pool.memset(ones[:], 0.0))
                for b in range(B):
                    pool.memset(ones[half_of(b), b:b + 1], 1.0).then_inc(zeroed, 1)
                    pool.memset(v[half_of(b), :, (1 - b) * HD:(2 - b) * HD], 0.0).then_inc(zeroed, 1)

            @block.scalar
            def _(act):
                def widen(u):
                    act.wait_ge(inv_ready, 1)
                    if u >= 2:
                        act.wait_ge(spread, u - 1)
                    act.copy(wide[:, u % 2, :].rearrange("p (n b d) -> p n b d", n=CB, b=B),
                             inv[:, CB * u:CB * u + CB, :].unsqueeze(3).broadcast_to((P, CB, B, HD))).then_inc(widened, 1)

                def output(u):
                    act.wait_ge(o_ready, u + 1)
                    for dst, src in out_quadrants(u):
                        op = act.copy(dst, src)
                    op.then_inc(o_act, 1)

                with act.Fori(0, 2 * WT // PASS) as i:
                    for n in range(PASS):
                        c.split_hi(act, A1_WK + n + 2, i * PASS)
                act.wait_ge(zeroed, 5)
                for n in range(WT):
                    act.wait_ge(v_ready, 2 * n + 1)
                    for dst, src in v_quadrants(BV + 2 * (n % 2), 2 * n):
                        op = act.copy(dst, src)
                    op.then_inc(v_act, 1)
                    c.split_hi(act, A1_WV + n + 2)
                    if n == SPREAD_AT - 1:
                        act.wait_ge(summed, 1)
                        act.activation(inv[:].rearrange("p n b -> p (n b)"), c.psum[:, BN, 0:UNITS * CB * B], ACT.Identity,
                                       bias=tiny[:]).then_inc(norm_out, 1)
                    if n >= SPREAD_AT:
                        widen(2 * (n - SPREAD_AT))
                        widen(2 * (n - SPREAD_AT) + 1)
                for u in range(4, UNITS):
                    widen(u)
                for u in range(0, UNITS, 2):
                    output(u)
                for n in range(WT):
                    if n == 0:
                        act.wait_ge(o_act, UNITS // 2)
                        act.wait_ge(o_dve, UNITS // 2)
                    if n >= 2:
                        c.wait_products(act, A1_WO + n - 2)
                    for b in range(B):
                        act.copy(part(ot_hi, n, b), of_tile(n, b)).then_inc(ot_hi_ready, 1)
                    if n >= 1:
                        c.split_hi(act, A1_WO + n + 1)
                c.split_hi(act, A1_WO + WT + 1)

            @block.vector
            def _(dve):
                own = c.dve_chain
                flat = k_acc[:].rearrange("p a d -> p (a d)")[:, 0:512]

                def divide(u):
                    dve.wait_ge(spread, u + 1)
                    some = q[:, unit(u), :].rearrange("p t i -> p (t i)")
                    dve.tensor_tensor(some, some, c.psum[:, BN + 1 - u % 2, :], ALU.mult).then_inc(divided, 1)

                def output(u):
                    dve.wait_ge(o_ready, u + 1)
                    for dst, src in out_quadrants(u):
                        op = dve.tensor_copy(dst, src)
                    op.then_inc(o_dve, 1)

                own.step(dve.memset(k_acc[:], 0.0))
                dve.sem_inc(k_free, 4)
                dve.sem_inc(q_free, 4)
                with dve.Fori(0, WT // PASS) as i:
                    own.enter(i, 2 * PASS)
                    for n in range(PASS):
                        for h in range(2):
                            dve.wait_ge(k_ready, i * (2 * PASS) + (2 * n + h + 1))
                            if h == 1:
                                dve.sem_inc(c.w_used, 1)
                            own.step(dve.scalar_tensor_tensor(flat, c.psum[:, BK + 2 * (n % 2) + h, :], 0.0, flat, ALU.max, ALU.add))
                            dve.sem_inc(k_free, 1)
                        c.split_lo(dve, A1_WK + n + 2, i * PASS)
                    own.leave(WT // PASS)
                own.step(dve.tensor_tensor(flat[:, 0:T], flat[:, 0:T], flat[:, T:2 * T], ALU.add))
                for x in range(2):
                    own.done(dve.tensor_copy(shift[half_of(x)], flat[half_of(1 - x), 0:T]))
                own.wait()
                own.step(dve.tensor_tensor(shift[:], shift[:], flat[:, 0:T], ALU.add))
                own.step(dve.tensor_scalar(ksum[:].rearrange("p b t -> p (b t)"), shift[:], HD ** -0.5, None, ALU.mult))
                with dve.Fori(0, WT // PASS) as i:
                    for n in range(PASS):
                        for h in range(2):
                            dve.wait_ge(q_ready, i * (2 * PASS) + (2 * n + h + 1))
                            if h == 1:
                                dve.sem_inc(c.w_used, 1)
                            src = chunks_of(BQ + 2 * (n % 2) + h)
                            for b in range(B):
                                to = q[half_of(b)].rearrange("p t (i g c e) -> p t i g c e", i=WT // PASS, g=2 * PASS, c=2)
                                for e in range(2):
                                    op = dve.scalar_tensor_tensor(
                                        to[:, :, bass.ds(i, 1), 2 * n + h, :, e].rearrange("p t a c -> p t (a c)"),
                                        src[half_of(e), b], 0.0,
                                        ksum[half_of(e), b, :].unsqueeze(2).broadcast_to((HD, P, 2)), ALU.max, ALU.mult)
                            op.then_inc(q_free, 1)
                        c.split_lo(dve, A1_WQ + n + 2, i * PASS)
                dve.wait_ge(bias_ready, 16)
                for b in range(B):
                    own.done(dve.tensor_tensor(c.x[:, b, :], c.x[:, b, :], bias[:], ALU.add))
                own.wait()
                for n in range(WT):
                    dve.wait_ge(v_ready, 2 * n + 2)
                    dve.sem_inc(c.w_used, 1)
                    for dst, src in v_quadrants(BV + 2 * (n % 2) + 1, 2 * n + 1):
                        op = dve.tensor_copy(dst, src)
                    op.then_inc(v_dve, 1)
                    c.split_lo(dve, A1_WV + n + 2)
                    if n == SPREAD_AT - 1:
                        dve.wait_ge(norm_out, 1)
                        dve.reciprocal(inv[:], inv[:]).then_inc(inv_ready, 1)
                    if n >= SPREAD_AT:
                        divide(2 * (n - SPREAD_AT))
                        divide(2 * (n - SPREAD_AT) + 1)
                for u in range(4, UNITS):
                    divide(u)
                for u in range(1, UNITS, 2):
                    output(u)
                for n in range(WT):
                    for b in range(B):
                        dve.wait_ge(ot_hi_ready, B * n + b + 1)
                        dve.tensor_tensor(part(ot_lo, n, b), of_tile(n, b), part(ot_hi, n, b).bitcast(F32), ALU.subtract)\
                           .then_inc(ot_lo_ready, 1)
                    if n >= 1:
                        c.split_lo(dve, A1_WO + n + 1)
                c.wait_products(dve, A1_WO + WT - 1)
                for b in range(B):
                    dve.tensor_tensor(c.x[:, b, :], c.x[:, b, :], c.psum[:, BY + b, :], ALU.add).then_inc(y_out, 1)
                dve.wait_ge(y_out, B)

            @block.tensor
            def _(pe):
                def heads(tile, banks, ready, i=0):
                    pe.wait_ge(c.lo_ready, i + (tile + 1))
                    slot = c.slot(tile)
                    for h in range(2):
                        for x in range(2):
                            yield h, x
                            w = slice((2 * h + x) * P, (2 * h + x + 1) * P)
                            for k in range(KC):
                                mm = three_passes(pe, c.psum[:, banks + h, T * x:T * x + T],
                                                  (c.w_hi[:, slot, k, w], c.w_lo[:, slot, k, w]),
                                                  (c.xt_hi[:, k, :], c.xt_lo[:, k, :]), k == 0, k == KC - 1)
                        mm.then_inc(ready, 1)

                def spread_out(u):
                    pe.wait_ge(widened, u + 1)
                    if u >= 2:
                        pe.wait_ge(divided, u - 1)
                    for x in range(CB):
                        mm = pe.matmul(c.psum[:, BN + 1 - u % 2, x * P:(x + 1) * P], wide[:, u % 2, x * P:(x + 1) * P],
                                       c.ident[:], start=True, stop=True)
                    mm.then_inc(spread, 1)

                for first, banks, ready, free in ((A1_WK, BK, k_ready, k_free), (A1_WQ, BQ, q_ready, q_free)):
                    with pe.Fori(0, WT // PASS) as i:
                        for n in range(PASS):
                            for h, x in heads(first + n, banks + 2 * (n % 2), ready, i * PASS):
                                if x == 0:
                                    pe.wait_ge(free, i * (2 * PASS) + (2 * n + h + 1))
                pe.wait_ge(zeroed, 5)
                chunk = 0
                for n in range(WT):
                    for h, x in heads(A1_WV + n, BV + 2 * (n % 2), v_ready):
                        if x == 0:
                            if n >= 2:
                                pe.wait_ge((v_act, v_dve)[h], n - 1)
                            else:
                                pe.wait_ge(k_free, 2 * WT + 2 * n + h + 1)
                        if SUMS_AT <= n < SPREAD_AT:
                            if chunk == 0:
                                pe.wait_ge(q_free, 2 * WT + 4)
                            for _ in range(UNITS * CB // (4 * (SPREAD_AT - SUMS_AT))):
                                mm = pe.matmul(c.psum[:, BN, B * chunk:B * chunk + B],
                                               q[:, P // HD * chunk:P // HD * (chunk + 1), :].rearrange("p t i -> p (t i)"),
                                               ones[:], start=True, stop=True)
                                chunk += 1
                            if chunk == UNITS * CB:
                                mm.then_inc(summed, 1)
                    if n >= SPREAD_AT:
                        spread_out(2 * (n - SPREAD_AT))
                        spread_out(2 * (n - SPREAD_AT) + 1)
                for u in range(4, UNITS):
                    spread_out(u)
                pe.wait_ge(v_act, WT)
                pe.wait_ge(v_dve, WT)
                for u in range(UNITS):
                    pe.wait_ge(divided, u + 1)
                    if u >= 4:
                        pe.wait_ge((o_act, o_dve)[u % 2], u // 2 - 1)
                    for x in range(TU):
                        t = TU * u + x
                        mm = pe.matmul(c.psum[:, BO + u % 4, HD * x:HD * x + HD], v[:, t, :], q[:, t, :], start=True, stop=True)
                    mm.then_inc(o_ready, 1)
                for n in range(WT):
                    slot = c.slot(A1_WO + n)
                    pe.wait_ge(c.lo_ready, A1_WO + n + 1)
                    pe.wait_ge(ot_lo_ready, B * n + B)
                    for b in range(B):
                        for k in range(KC):
                            mm = three_passes(pe, c.psum[:, BY + b, :], (ot_hi[:, n % 2, k, b, :], ot_lo[:, n % 2, k, b, :]),
                                              (c.w_hi[:, slot, k, :], c.w_lo[:, slot, k, :]),
                                              n == k == 0, n == WT - 1 and k == KC - 1)
                    mm.then_inc(c.w_used, 1)


def experts_1(c, given):
    nc = c.nc
    W1, W2 = 4, 4
    PER = W1 + W2
    BH, BY = 0, 4

    with ExitStack() as ctx:
        def sb(name, shape, dt=F32):
            return ctx.enter_context(nc.sbuf_tensor(f"f1_{name}", shape, dt))

        def sem(name):
            return c.layer_sem(f"f1_{name}")

        gates = sb("gates", [P, B, E])
        gate(c, "f1", gates, 1, given)

        b1 = sb("b1", [P, E, 4 * W1])
        h = sb("h", [P, 2, 4, T])
        h_hi = sb("h_hi", [P, 4 * W1, T], F32R)
        h_lo = sb("h_lo", [P, 4 * W1, T], F32R)
        b1_ready, relu_act, relu_dve = sem("b1_ready"), sem("relu_act"), sem("relu_dve")
        hi_ready, lo_ready, y_free = sem("h_hi_ready"), sem("h_lo_ready"), sem("ey_free")

        def expert(up, down, e, i):
            for t in range(W1):
                up(e, t, F1_W + W1 + 2 * t, i)
                down(e - 1, t, F1_W + W1 + 2 * t + 1, i)

        LAST = F1_W + W1 + PER * (E - 1)

        with nc.Block(no_gpsimd_drain=True) as block:

            @block.sync
            def _(sp):
                sp.dma_start(b1[:], c.dram["f1_b1"]).then_inc(b1_ready, 16)
                with sp.Fori(0, (PER * E - RAW) // RAW) as j:
                    for n in range(RAW):
                        c.load_weight(sp, F1_W + RAW + n, j * RAW)

            @block.scalar
            def _(act):
                def high(s, t):
                    act.wait_ge(relu_act, s * 2 + 2)
                    act.wait_ge(relu_dve, s * 2 + 2)
                    act.copy(h_hi[:, 4 * t:4 * t + 4, :], h[:, t % 2]).then_inc(hi_ready, 1)

                def up(e, t, tile, i, split=True):
                    s, q = e * W1 + t, t % 2
                    if split:
                        c.split_hi(act, tile + 2, i)
                    c.wait_products(act, tile, i)
                    if t > 1 or not isinstance(e, int) or e > 0:
                        act.wait_ge(lo_ready, s - 1)
                    at = e if isinstance(e, int) else bass.ds(e, 1)
                    for x in range(2, 4):
                        act.activation(h[:, q, x, :], c.psum[:, BH + 2 * q + 1, T * (x - 2):T * (x - 1)], ACT.Relu,
                                       bias=b1[:, at, 4 * t + x:4 * t + x + 1]).then_inc(relu_act, 1)
                    if t > 0 or not isinstance(e, int) or e > 0:
                        high(s - 1, (t - 1) % W1)

                def down(e, t, tile, i):
                    c.split_hi(act, tile + 2, i)

                act.wait_ge(b1_ready, 16)
                for t in range(W1):
                    up(0, t, F1_W + t, 0)
                with act.Fori(0, E - 1) as e:
                    expert(up, down, e + 1, e * PER)
                high(E * W1 - 1, W1 - 1)
                for t in range(W2 - 2):
                    down(E - 1, t, LAST + t, 0)

            @block.vector
            def _(dve):
                def low(s, t):
                    dve.wait_ge(hi_ready, s + 1)
                    dve.tensor_tensor(h_lo[:, 4 * t:4 * t + 4, :], h[:, t % 2], h_hi[:, 4 * t:4 * t + 4, :].bitcast(F32),
                                      ALU.subtract).then_inc(lo_ready, 1)

                def up(e, t, tile, i):
                    s, q = e * W1 + t, t % 2
                    c.wait_products(dve, tile, i)
                    if t > 1 or not isinstance(e, int) or e > 0:
                        dve.wait_ge(lo_ready, s - 1)
                    at = e if isinstance(e, int) else bass.ds(e, 1)
                    for x in range(2):
                        dve.tensor_scalar(h[:, q, x, :], c.psum[:, BH + 2 * q, T * x:T * x + T],
                                          b1[:, at, 4 * t + x:4 * t + x + 1], 0.0, ALU.add, ALU.max).then_inc(relu_dve, 1)
                    c.split_lo(dve, tile + 2, i)
                    if t > 0 or not isinstance(e, int) or e > 0:
                        low(s - 1, (t - 1) % W1)

                def down(e, t, tile, i):
                    if t == W2 - 1:
                        c.wait_products(dve, tile, i)
                        at = slice(e, e + 1) if isinstance(e, int) else bass.ds(e, 1)
                        for b in range(B):
                            dve.scalar_tensor_tensor(c.x[:, b, :], c.psum[:, BY + b, :], gates[:, b, at], c.x[:, b, :],
                                                     ALU.mult, ALU.add).then_inc(y_free, 1)
                        dve.wait_ge(y_free, e * B + 2 * B)
                    if not (isinstance(e, int) and t >= W2 - 2):
                        c.split_lo(dve, tile + 2, i)

                dve.wait_ge(b1_ready, 16)
                for t in range(W1):
                    up(0, t, F1_W + t, 0)
                with dve.Fori(0, E - 1) as e:
                    expert(up, down, e + 1, e * PER)
                low(E * W1 - 1, W1 - 1)
                for t in range(W2):
                    down(E - 1, t, LAST + t, 0)

            @block.tensor
            def _(pe):
                pe.sem_inc(y_free, B)

                def up(e, t, tile, i):
                    s, slot = e * W1 + t, c.slot(tile)
                    pe.wait_ge(c.lo_ready, i + (tile + 1))
                    if not isinstance(e, int) or s >= 2:
                        pe.wait_ge(relu_dve, s * 2 - 2)
                        pe.wait_ge(relu_act, s * 2 - 2)
                    for x in range(4):
                        w = slice(x * P, (x + 1) * P)
                        for k in range(KC):
                            mm = three_passes(pe, c.psum[:, BH + 2 * (t % 2) + x // 2, T * (x % 2):T * (x % 2) + T],
                                              (c.w_hi[:, slot, k, w], c.w_lo[:, slot, k, w]),
                                              (c.xt_hi[:, k, :], c.xt_lo[:, k, :]), k == 0, k == KC - 1)
                    mm.then_inc(c.w_used, 1)

                def down(e, t, tile, i):
                    slot = c.slot(tile)
                    pe.wait_ge(c.lo_ready, i + (tile + 1))
                    pe.wait_ge(lo_ready, e * W1 + (t + 1))
                    if t == 0:
                        pe.wait_ge(y_free, e * B + B)
                    for b in range(B):
                        cols = slice(b * P, (b + 1) * P)
                        for k in range(KC):
                            mm = three_passes(pe, c.psum[:, BY + b, :], (h_hi[:, KC * t + k, cols], h_lo[:, KC * t + k, cols]),
                                              (c.w_hi[:, slot, k, :], c.w_lo[:, slot, k, :]),
                                              t == k == 0, t == W2 - 1 and k == KC - 1)
                    mm.then_inc(c.w_used, 1)

                for t in range(W1):
                    up(0, t, F1_W + t, 0)
                with pe.Fori(0, E - 1) as e:
                    expert(up, down, e + 1, e * PER)
                for t in range(W2):
                    down(E - 1, t, LAST + t, 0)


def perceiver(nc, dram, out):
    with ExitStack() as ctx:
        c = Core(nc, ctx, dram)
        with ExitStack() as early:
            glance = early.enter_context(nc.sbuf_tensor("x0_glance", [P, B, GLANCE, D], F32, side="right"))
            with nc.sbuf_tensor("n0_col", [P, 2, KC], F32) as n0_col:
                n0_cols = c.layer_sem("n0_cols")
                constants(c, glance, n0_col, n0_cols)
                normalize(c, "n0", given=(n0_col, n0_cols), twice=True)
            cross_attention_0(c, early, glance)
        normalize(c, "n1", owed=A0_WQK + 1)
        self_attention_0(c)
        with ExitStack() as inner:
            given = GateInputs(c, inner, "f0", bias=True)
            normalize(c, "n2", dram["norm_scale"], rms=True, loads=given.loads, owed=F0_W + 1)
            experts_0(c, given)
        c.free_semaphores()
        normalize(c, "n3")
        cross_attention_1(c)
        normalize(c, "n4", owed=A1_WK + 1)
        linear_attention_1(c)
        with ExitStack() as inner:
            given = GateInputs(c, inner, "f1")
            normalize(c, "n5", loads=given.loads, owed=F1_W + 1)
            experts_1(c, given)
        stored = ctx.enter_context(nc.semaphore("stored"))
        with nc.Block(no_gpsimd_drain=True) as block:

            @block.sync
            def _(sp):
                sp.dma_start(out.rearrange("b p d -> p b d"), c.x[:]).then_inc(stored, 16)
                sp.wait_ge(stored, 16)


def lay_out(inputs):
    import numpy as np

    def tiles(w):
        k, n = w.shape
        w = w.reshape(k // D, KC, P, n // D, D)
        return w.transpose(3, 0, 2, 1, 4).reshape(-1, P, KC * D)

    def columns(v):
        return np.ascontiguousarray(np.moveaxis(v.reshape(*v.shape[:-1], -1, P), -1, 0))

    i = {name: np.asarray(a) for name, a in inputs.items()}

    def halves(w):
        return np.moveaxis(w.reshape(*w.shape[:-1], -1, P, 2), -1, -2).reshape(w.shape)

    def among(ups, downs):
        order = [ups[0]]
        for up, down in zip(ups[1:], downs[:-1]):
            for t in range(len(up)):
                order += [up[t:t + 1], down[t:t + 1]]
        return order + [downs[-1]]

    parts = [tiles(i["L0_xattn_Wq"]), tiles(i["L0_xattn_Wkv"]), tiles(i["L0_xattn_Wo"]),
             tiles(i["L0_attn_Wc"].T), tiles(i["L0_attn_Wo"].T)]
    parts += among([tiles(halves(w)) for w in i["L0_ffn_mlp1_w"]], [tiles(w) for w in i["L0_ffn_mlp2_w"]])
    parts += [tiles(i[f"L1_xattn_{n}"]) for n in ("Wq", "Wk", "Wv", "Wo")]
    parts += [tiles(i[f"L1_attn_{n}"]) for n in ("Wk", "Wq", "Wv", "Wo")]
    parts += among([tiles(w) for w in i["L1_ffn_w1"]], [tiles(w) for w in i["L1_ffn_w2"]])
    weights = np.concatenate(parts)
    assert len(weights) == TILES
    return {
        "x": i["x"], "ctx": i["ctx_1024"], "cos": i["L0_xattn_cos"], "sin": i["L0_xattn_sin"], "weights": weights,
        "ln_lat_g": columns(i["L0_xattn_ln_lat_g"]), "ln_lat_b": columns(i["L0_xattn_ln_lat_b"]),
        "ln_ctx_g": columns(i["L0_xattn_ln_ctx_g"]), "ln_ctx_b": columns(i["L0_xattn_ln_ctx_b"]),
        "x0_bo": i["L0_xattn_bo"], "a0_bqk": columns(i["L0_attn_bc"][:2 * D]), "a0_bv": i["L0_attn_bc"][2 * D:],
        "a0_bo": i["L0_attn_bo"], "norm_scale": columns(i["L0_ffn_norm_scale"]),
        "f0_gate_w": np.ascontiguousarray(np.moveaxis(i["L0_ffn_gate_w"].reshape(KC, P, E), 1, 0)),
        "f0_gate_b": i["L0_ffn_gate_b"], "f0_b1": columns(halves(i["L0_ffn_mlp1_b"])), "f0_b2": i["L0_ffn_mlp2_b"],
        "x1_bq": columns(i["L1_xattn_bq"]), "x1_bk": columns(i["L1_xattn_bk"]), "x1_bv": i["L1_xattn_bv"],
        "x1_bo": i["L1_xattn_bo"], "a1_bo": i["L1_attn_bo"],
        "f1_gate_w": np.ascontiguousarray(np.moveaxis(i["L1_ffn_gate_w"].T.reshape(KC, P, E), 1, 0)),
        "f1_b1": columns(i["L1_ffn_b1"]), "f1_b2": i["L1_ffn_b2"],
    }


def kernel(**inputs):
    import numpy as np
    import concourse.bacc as bacc
    from concourse.bass_utils import run_bass_kernel_spmd

    nc = bacc.Bacc("TRN2", target_bir_lowering=False, num_devices=1)
    arrays = {f"in_{name}": np.ascontiguousarray(a) for name, a in lay_out(inputs).items()}
    dram = {name.removeprefix("in_"): nc.dram_tensor(name, a.shape, mybir.dt.from_np(a.dtype), kind="ExternalInput").ap()
            for name, a in arrays.items()}
    out = nc.dram_tensor("out", (B, P, D), F32, kind="ExternalOutput").ap()
    perceiver(nc, dram, out)
    run = run_bass_kernel_spmd(nc, [arrays], core_ids=[0])
    return run.results[0]["out"]
```
